# Optimizing a Trainium2 kernel written in Bass

```python
import numpy as np
import jax
import jax.numpy as jnp

def _softmax(x, axis=-1):
    return jax.nn.softmax(x, axis=axis)

def _gelu(x):
    return jax.nn.gelu(x, approximate=True)

def _silu(x):
    return jax.nn.silu(x)

def _sigmoid(x):
    return jax.nn.sigmoid(x)

def _layernorm(x, axis=-1, eps=1e-05):
    m = jnp.mean(x, axis=axis, keepdims=True)
    v = jnp.var(x, axis=axis, keepdims=True)
    return (x - m) / jnp.sqrt(v + eps)

def _scatter_add(tgt, idx, src, axis=0):
    return tgt.at[idx].add(src)

def _segment_sum(src, seg, n):
    return jax.ops.segment_sum(src, seg, n)
kernel_name = 'mk_recurrent_d1_jaxref_r8_108117'

def setup_inputs(seed: int=0):
    np.random.seed(seed)
    _w = jnp.asarray

    def _L0_attn_setup():
        import jax, jax.numpy as jnp
        import numpy as np
        D_MODEL = 128
        N_HEADS = 16
        D_LATENT = 32
        HEAD_DIM = D_MODEL // N_HEADS

        def apply_rope(x):
            B, T, H, D = x.shape
            inv_freq = 1.0 / 10000.0 ** (jnp.arange(0, D, 2, dtype=jnp.float32) / D)
            t = jnp.arange(T, dtype=jnp.float32)
            freqs = t[:, None] * inv_freq[None, :]
            sin_f = jnp.sin(freqs)[None, :, None, :]
            cos_f = jnp.cos(freqs)[None, :, None, :]
            x1, x2 = jnp.split(x, 2, axis=-1)
            return jnp.concatenate([x1 * cos_f - x2 * sin_f, x1 * sin_f + x2 * cos_f], axis=-1)
        key = jax.random.key(seed)
        ks = jax.random.split(key, 10)
        B, T = (4, 512)
        s = lambda fan_in: 1.0 / np.sqrt(fan_in)
        return {'x': jax.random.normal(ks[0], (B, T, D_MODEL), dtype=jnp.float32), 'Wq': jax.random.normal(ks[1], (D_MODEL, D_MODEL), dtype=jnp.float32) * s(D_MODEL), 'bq': jnp.zeros((D_MODEL,), jnp.float32), 'Wdown': jax.random.normal(ks[2], (D_MODEL, D_LATENT), dtype=jnp.float32) * s(D_MODEL), 'bdown': jnp.zeros((D_LATENT,), jnp.float32), 'Wup': jax.random.normal(ks[3], (D_LATENT, 2 * D_MODEL), dtype=jnp.float32) * s(D_LATENT), 'bup': jnp.zeros((2 * D_MODEL,), jnp.float32), 'Wout': jax.random.normal(ks[4], (D_MODEL, D_MODEL), dtype=jnp.float32) * s(D_MODEL), 'bout': jnp.zeros((D_MODEL,), jnp.float32)}
    _L0_attn_in = _L0_attn_setup()

    def _L0_ffn_setup():
        import jax, jax.numpy as jnp
        import numpy as np
        NH, NKV, E, K = (16, 4, 8, 2)
        CAP_FACTOR = 1.25
        LN_EPS = 1e-05

        def _layer_norm(x, w, b):
            mu = jnp.mean(x, axis=-1, keepdims=True)
            var = jnp.mean(jnp.square(x - mu), axis=-1, keepdims=True)
            return (x - mu) * jax.lax.rsqrt(var + LN_EPS) * w + b
        key = jax.random.key(seed)
        ks = jax.random.split(key, 6)
        S, B, H, F = (256, 1, 128, 256)
        HD = H // NH
        qkv_out = NKV * (NH // NKV + 2) * HD
        f32 = jnp.float32
        return {'hidden_states': jax.random.normal(ks[0], (S, B, H), f32), 'ln1_weight': jnp.ones((H,), f32), 'ln1_bias': jnp.zeros((H,), f32), 'ln2_weight': jnp.ones((H,), f32), 'ln2_bias': jnp.zeros((H,), f32), 'qkv_weight': jax.random.normal(ks[1], (qkv_out, H), f32) * 0.02, 'proj_weight': jax.random.normal(ks[2], (H, H), f32) * 0.02, 'router_weight': jax.random.normal(ks[3], (H, E), f32) * 0.02, 'moe_w1': jax.random.normal(ks[4], (E, H, F), f32) * 0.02, 'moe_w2': jax.random.normal(ks[5], (F and E, F, H), f32)[:E] * 0.02 if False else jax.random.normal(ks[5], (E, F, H), f32) * 0.02}
    _L0_ffn_in = _L0_ffn_setup()
    _d = {'L0_attn_x': _L0_attn_in['x'], 'L0_attn_Wq': _L0_attn_in['Wq'], 'L0_attn_bq': _L0_attn_in['bq'], 'L0_attn_Wdown': _L0_attn_in['Wdown'], 'L0_attn_bdown': _L0_attn_in['bdown'], 'L0_attn_Wup': _L0_attn_in['Wup'], 'L0_attn_bup': _L0_attn_in['bup'], 'L0_attn_Wout': _L0_attn_in['Wout'], 'L0_attn_bout': _L0_attn_in['bout'], 'L0_ffn_ln1_weight': _L0_ffn_in['ln1_weight'], 'L0_ffn_ln1_bias': _L0_ffn_in['ln1_bias'], 'L0_ffn_ln2_weight': _L0_ffn_in['ln2_weight'], 'L0_ffn_ln2_bias': _L0_ffn_in['ln2_bias'], 'L0_ffn_qkv_weight': _L0_ffn_in['qkv_weight'], 'L0_ffn_proj_weight': _L0_ffn_in['proj_weight'], 'L0_ffn_router_weight': _L0_ffn_in['router_weight'], 'L0_ffn_moe_w1': _L0_ffn_in['moe_w1'], 'L0_ffn_moe_w2': _L0_ffn_in['moe_w2']}
    _x0 = _d['L0_attn_x']
    _d['L0_attn_x'] = jax.random.normal(jax.random.fold_in(jax.random.key(seed), 1), (8, 512, 128), dtype=_x0.dtype)
    del _x0
    return _d

def reference(L0_attn_x, L0_attn_Wq, L0_attn_bq, L0_attn_Wdown, L0_attn_bdown, L0_attn_Wup, L0_attn_bup, L0_attn_Wout, L0_attn_bout, L0_ffn_ln1_weight, L0_ffn_ln1_bias, L0_ffn_ln2_weight, L0_ffn_ln2_bias, L0_ffn_qkv_weight, L0_ffn_proj_weight, L0_ffn_router_weight, L0_ffn_moe_w1, L0_ffn_moe_w2):

    def _L0_attn_ref(x, Wq, bq, Wdown, bdown, Wup, bup, Wout, bout):
        import jax, jax.numpy as jnp
        import numpy as np
        D_MODEL = 128
        N_HEADS = 16
        D_LATENT = 32
        HEAD_DIM = D_MODEL // N_HEADS

        def apply_rope(x):
            B, T, H, D = x.shape
            inv_freq = 1.0 / 10000.0 ** (jnp.arange(0, D, 2, dtype=jnp.float32) / D)
            t = jnp.arange(T, dtype=jnp.float32)
            freqs = t[:, None] * inv_freq[None, :]
            sin_f = jnp.sin(freqs)[None, :, None, :]
            cos_f = jnp.cos(freqs)[None, :, None, :]
            x1, x2 = jnp.split(x, 2, axis=-1)
            return jnp.concatenate([x1 * cos_f - x2 * sin_f, x1 * sin_f + x2 * cos_f], axis=-1)
        B, T, D = x.shape
        H, Dh = (N_HEADS, HEAD_DIM)
        q = x @ Wq + bq
        kv_latent = x @ Wdown + bdown
        kv = kv_latent @ Wup + bup
        q = q.reshape(B, T, H, Dh)
        kv = kv.reshape(B, T, H, 2 * Dh)
        k, v = jnp.split(kv, 2, axis=-1)
        q = apply_rope(q)
        k = apply_rope(k)
        att = jnp.einsum('bthd,btgd->bthg', q, k) / jnp.sqrt(jnp.float32(Dh))
        att = jax.nn.softmax(att, axis=-1)
        out = jnp.einsum('bthg,btgd->bthd', att, v)
        out = out.reshape(B, T, D)
        return out @ Wout + bout

    def _L0_ffn_ref(hidden_states, ln1_weight, ln1_bias, ln2_weight, ln2_bias, qkv_weight, proj_weight, router_weight, moe_w1, moe_w2):
        import jax, jax.numpy as jnp
        import numpy as np
        NH, NKV, E, K = (16, 4, 8, 2)
        CAP_FACTOR = 1.25
        LN_EPS = 1e-05

        def _layer_norm(x, w, b):
            mu = jnp.mean(x, axis=-1, keepdims=True)
            var = jnp.mean(jnp.square(x - mu), axis=-1, keepdims=True)
            return (x - mu) * jax.lax.rsqrt(var + LN_EPS) * w + b
        S, B, H = hidden_states.shape
        HD = H // NH
        q_per_kv = NH // NKV
        ln1 = _layer_norm(hidden_states, ln1_weight, ln1_bias)
        qkv = jnp.einsum('sbh,oh->sbo', ln1, qkv_weight)
        qkv = qkv.reshape(S, B, NKV, (q_per_kv + 2) * HD)
        q = qkv[..., :q_per_kv * HD].reshape(S, B, NH, HD)
        k = qkv[..., q_per_kv * HD:(q_per_kv + 1) * HD]
        v = qkv[..., (q_per_kv + 1) * HD:]
        qb = jnp.transpose(q, (1, 2, 0, 3)).reshape(B, NKV, q_per_kv, S, HD)
        kb = jnp.transpose(k, (1, 2, 0, 3))
        vb = jnp.transpose(v, (1, 2, 0, 3))
        scale = 1.0 / np.sqrt(HD).astype(np.float32)
        scores = jnp.einsum('bgqsd,bgtd->bgqst', qb, kb) * scale
        causal = jnp.tril(jnp.ones((S, S), bool))
        scores = jnp.where(causal, scores, jnp.finfo(scores.dtype).min)
        attn = jax.nn.softmax(scores, axis=-1)
        ao = jnp.einsum('bgqst,bgtd->bgqsd', attn, vb)
        ao = ao.reshape(B, NH, S, HD)
        ao = jnp.transpose(ao, (2, 0, 1, 3)).reshape(S, B, H)
        proj = jnp.einsum('sbh,oh->sbo', ao, proj_weight)
        h1 = hidden_states + proj
        ln2 = _layer_norm(h1, ln2_weight, ln2_bias)
        x = ln2.reshape(-1, H)
        N = x.shape[0]
        logits = x @ router_weight
        probs = jax.nn.softmax(logits, axis=-1)
        top_p, top_i = jax.lax.top_k(probs, K)
        top_p = top_p / jnp.sum(top_p, axis=-1, keepdims=True)
        exp_idx = top_i.reshape(-1)
        exp_p = top_p.reshape(-1)
        order = jnp.argsort(exp_idx, stable=True)
        sorted_exp = exp_idx[order]
        counts = jnp.bincount(exp_idx, length=E)
        offsets = jnp.concatenate([jnp.zeros((1,), counts.dtype), jnp.cumsum(counts)[:-1]])
        within = jnp.arange(N * K) - offsets[sorted_exp]
        cap = int(np.ceil(N * K / E * CAP_FACTOR))
        T = E * cap
        valid = within < cap
        dst = jnp.where(valid, sorted_exp * cap + within, T)
        padded_tokens = jnp.zeros((T, H), x.dtype).at[dst].set(x[order // K], mode='drop')
        padded_probs = jnp.zeros((T,), exp_p.dtype).at[dst].set(exp_p[order], mode='drop')
        padded_tid = jnp.zeros((T,), jnp.int32).at[dst].set((order // K).astype(jnp.int32), mode='drop')
        xt = padded_tokens.reshape(E, cap, H)
        fc1 = jax.nn.gelu(jnp.einsum('ech,ehf->ecf', xt, moe_w1))
        fc2 = jnp.einsum('ecf,efh->ech', fc1, moe_w2).reshape(T, H)
        weighted = fc2 * padded_probs[:, None]
        moe_out = jnp.zeros((N, H), hidden_states.dtype).at[padded_tid].add(weighted)
        return h1 + moe_out.reshape(S, B, H)
    x = L0_attn_x
    xn = _layernorm(x, axis=-1)
    s = _L0_attn_ref(xn, L0_attn_Wq, L0_attn_bq, L0_attn_Wdown, L0_attn_bdown, L0_attn_Wup, L0_attn_bup, L0_attn_Wout, L0_attn_bout)
    g = _silu(_L0_ffn_ref(xn, L0_ffn_ln1_weight, L0_ffn_ln1_bias, L0_ffn_ln2_weight, L0_ffn_ln2_bias, L0_ffn_qkv_weight, L0_ffn_proj_weight, L0_ffn_router_weight, L0_ffn_moe_w1, L0_ffn_moe_w2))
    x = x + s * g
    return x

_drawn_inputs = setup_inputs


def setup_inputs(seed=0):
    import zlib

    import numpy as np

    out = dict(_drawn_inputs(seed))
    spreads = {'L0_attn_bq': (0.0, 0.472),
     'L0_attn_bdown': (0.0, 0.282),
     'L0_attn_bup': (0.0, 0.291),
     'L0_attn_bout': (0.0, 0.1),
     'L0_ffn_ln1_weight': (1.0, 0.6),
     'L0_ffn_ln1_bias': (0.0, 0.8),
     'L0_ffn_ln2_weight': (1.0, 0.6),
     'L0_ffn_ln2_bias': (0.0, 0.8)}
    factors = {'L0_ffn_qkv_weight': 6.983,
     'L0_ffn_proj_weight': 6.897,
     'L0_ffn_router_weight': 8.0,
     'L0_ffn_moe_w1': 8.0,
     'L0_ffn_moe_w2': 8.0}
    for name, (base, spread) in spreads.items():
        noise = np.random.default_rng([zlib.crc32(name.encode()), seed]).standard_normal(out[name].shape)
        drawn = base * np.exp(spread * noise) if base else spread * noise
        out[name] = jnp.asarray(drawn.astype(out[name].dtype))
    for name, factor in factors.items():
        out[name] = (out[name] * factor).astype(out[name].dtype)
    return out
```

```python
from contextlib import ExitStack

import numpy as np

import concourse.bass as bass
from concourse import mybir

F32 = mybir.dt.float32
BF16 = mybir.dt.bfloat16
U32 = mybir.dt.uint32
ALU = mybir.AluOpType
ACT = mybir.ActivationFunctionType
AX_X = mybir.AxisListType.X

P = 128
S, T, D = 8, 512, 128
TT = T // P
NT = S * TT
H, HD = 16, 8
LAT = 32
G, QH = 4, 4
GW = (QH + 2) * HD
QKV = G * GW
E, FF, TOPK = 8, 256, 2
FH = FF // P
CAP = int(np.ceil(S * T * TOPK / E * 1.25))
CT = CAP // P
SLOTS = E * CAP
EPS = 1e-5
SCALE = float(1.0 / np.sqrt(np.float32(HD)))
NEG = -3.0e38
CHUNK = S // 2
HELPED = 2


def build(nc, x, wq, bq, wdown, bdown, wupk, wupv, wout, bout, ln1w, ln1b, ln2w, ln2b,
          wqkv, wproj, wrouter, w1, w2, cos, sin, identf, ones1, tri, allones, rev8, ebase, dump, out):
    slots_d = nc.dram_tensor("slot_rows", (SLOTS + S * T * TOPK, D), F32, kind="Internal").ap()
    expert_d = nc.dram_tensor("expert_rows", (SLOTS, D), F32, kind="Internal").ap()

    with ExitStack() as ctx:
        def sb(name, shape, dt=F32):
            return ctx.enter_context(nc.sbuf_tensor(name, shape, dt))

        def ps(name, shape, dt=F32):
            return ctx.enter_context(nc.psum_tensor(name, shape, dt))

        def sem(name):
            return ctx.enter_context(nc.semaphore(name))

        def room(of, at, *shape):
            n = int(np.prod(shape))
            names = [f"a{k}" for k in range(len(shape))]
            return of[:, at:at + n].rearrange(f"p ({' '.join(names)}) -> p {' '.join(names)}", **dict(zip(names, shape)))

        given = dict(identf=identf, ln1w=ln1w, ln1b=ln1b, wqkv=wqkv, wdown=wdown, bdown=bdown, wq=wq, bq=bq, ones1=ones1,
                     wupk=wupk, wupv=wupv, cos=cos, sin=sin, wproj=wproj, ln2w=ln2w, ln2b=ln2b, wrouter=wrouter,
                     wout=wout, bout=bout.partition_broadcast(P), rev8=rev8, ebase=ebase, dump=dump, tri=tri, allones=allones)
        sizes = dict(identf=[P, P], ln1w=[P, 1], ln1b=[P, 1], wqkv=[P, QKV], wdown=[P, LAT], bdown=[LAT, 1], wq=[P, D], bq=[1, D],
                     ones1=[1, P], wupk=[LAT + 1, D], wupv=[LAT + 1, D], cos=[P, TT * D], sin=[P, TT * D], wproj=[P, D],
                     ln2w=[P, 1], ln2b=[P, 1], wrouter=[P, E], wout=[P, D], bout=[P, D], rev8=[P, E], ebase=[P, E],
                     dump=[P, TOPK * NT], tri=[P, P], allones=[P, P])
        C = {n: sb("c_" + n, sizes[n], BF16 if n in ("tri", "allones") else F32) for n in given}

        xn_all = sb("xn_all", [P, S, TT, D])
        qkv_all = sb("qkv_all", [P, S, TT * QKV])
        qkv_t = qkv_all[:].rearrange("p s (a c) -> p s a c", a=TT)
        z2_all = qkv_all[:, :, 0:TT * D].rearrange("p s (a d) -> p s a d", a=TT)
        q_all = sb("q_all", [P, S, TT * D])
        k_all = sb("k_all", [P, S, TT * D])
        v_all = sb("v_all", [P, S, TT * D])
        prodA = sb("prodA", [P, 2, 2048])
        prodB = sb("prodB", [P, 2, 2048])
        score = sb("score", [P, 2, TT * H * H])
        hmax = sb("hmax", [P, 2, TT * H])
        hsum = sb("hsum", [P, 2, TT * H])
        ao = sb("ao", [P, 2, TT, D])
        stat = sb("stat", [P, NT, 6])
        mom = sb("mom", [P, 6, NT])
        eps = sb("eps", [P, 1])
        zeros = sb("zeros", [P, 1, D])

        flat = sb("flat", [P, 8 * CAP])
        xnb = room(flat, 0, 2, TT, D)
        zb = room(flat, 1024, 2, TT, D)
        xnT = room(flat, 2048, 2, T)
        lnT = room(flat, 3072, 2, T)
        latT = room(flat, 4096, 2, T)
        aoc = room(flat, 5120, 2, TT, D)
        bT = room(flat, 6144, T)
        t1 = room(flat, 6656, 2, TT * D)
        t2 = room(flat, 7680, 2, TT * D)
        t3 = room(flat, 8704, 2, TT * D)
        turned_k = ((t1[:, 1], t2[:, 1]), (t3[:, 0], t3[:, 1]))
        xe = room(flat, 0, 2, CT, D)
        xeT = room(flat, 2 * CAP, CAP)
        hT = room(flat, 3 * CAP, FH, CAP)
        ye = room(flat, 5 * CAP, 2, CT, D)
        w1_sb = room(flat, 7 * CAP, 2, FF)
        w2_sb = room(flat, 7 * CAP + 2 * FF, 2, FH, D)
        yg = room(flat, 0, 2, TT, TOPK, D)
        fb = room(flat, 2048, 2, TT, D)
        gb = room(flat, 3072, 2, TT, D)
        xr = room(flat, 4096, 2, TT, D)
        aoT = sb("aoT", [P, T])

        prodqk = prodA[:].rearrange("p l (t s q d) -> p l t s q d", t=S, s=S, q=QH)
        prodpv = prodB[:].rearrange("p l (t s q d) -> p l t s q d", t=S, s=S, q=QH)
        sc = score[:, 0, 0:2 * S * S * QH].rearrange("p (l t s q) -> p l t s q", l=2, t=S, s=S)
        sc2 = score[:, 0, 2 * S * S * QH:].rearrange("p (l t s q) -> p l t s q", l=2, t=S, s=S)
        smax = hmax[:, 0, :].rearrange("p (l m) -> p l m", l=2)
        ssum = hsum[:, 0, :].rearrange("p (l m) -> p l m", l=2)

        logit = sb("logit", [P, NT, E])
        best = sb("best", [P, TOPK, NT])
        onehot = sb("onehot", [P, TOPK, NT, E])
        cum = sb("cum", [P, 2, NT, E])
        tmp8 = sb("tmp8", [P, NT, E])
        tmp1 = sb("tmp1", [P, NT])
        fit1 = sb("fit1", [P, NT])
        gate = sb("gate", [P, TOPK, NT])
        gate_s = sb("gate_s", [P, 2, TOPK, TT])
        mask16 = sb("mask16", [P, NT, E], BF16)
        gather_at = sb("gather_at", [P, TOPK, NT], U32)
        scatter_at = sb("scatter_at", [P, TOPK, NT], U32)

        bank = [ps(f"bank{i}", [P, T]) for i in range(8)]

        names = """consts_in filled
            moments norm1 norm2 dev_done xnb_done zb_done xnT_ready xnT_done zT_ready lnT_done lat_ready lat_done
            bqkv_ready bqkv_done q_ready q_read k_ready k_done v_ready v_done rope_q rope_k roped_k
            qk_prod qk_score s_max s_diff s_exp s_sum s_rsum s_prob pv_own pv_prod pv_sum
            aoc_done bT_ready bT_done proj_ready h1_done z2_done z2_kept z2T_ready x2T_done logit_ready logit_kept
            route diff_done route_exp mask_done pos_ready index_done zero_done zero_out scattered
            prod_done sum_done help_qk help_pv score_done row_max row_diff row_exp row_sum row_inv out_sum ao_done ao_ready aoT_done
            attn_ready attn_done
            xeT_ready xeT_done fc1_ready gelu_done fc2_ready ye_done
            gate_in f_step f_done silu_done gate_done res_done""".split()
        W = {n: sem(n) for n in names}
        x_in, w_in, xe_in, ye_out, gathered, tail_in, y_out = ([sem(f"{n}{i}") for i in range(2)] for n in (
            "x_in", "w_in", "xe_in", "ye_out", "gathered", "tail_in", "y_out"))
        block = ctx.enter_context(nc.Block())

        def ev(half, par):
            return 2 * half + par

        def after(half, par):
            return (half, 1) if par == 0 else (half + 1, 0)

        def wait_past(eng, name, count):
            if not isinstance(count, int) or count > 0:
                eng.wait_ge(W[name] if isinstance(name, str) else name, count)

        def staggered(eng, first, second):
            first(0, 0, False)
            first(0, 1, False)
            second(0, 0, False)
            first(1, 0, True)
            second(0, 1, False)
            with eng.Fori(1, S // 2 - 1) as half:
                for par in range(2):
                    first(*after(half, par), True)
                    second(half, par, True)
            first(S // 2 - 1, 1, True)
            second(S // 2 - 1, 0, True)
            second(S // 2 - 1, 1, True)

        def in_pairs(eng, body):
            body(0, 0, False)
            body(0, 1, False)
            with eng.Fori(1, S // 2) as half:
                for par in range(2):
                    body(half, par, True)
        n_consts = 16 * len(given)
        chunks = [(i, min(T, CAP - i)) for i in range(0, CAP, T)]

        def fourth(eng, expert, attention):
            def two_experts(half, par):
                expert(half, 0)
                expert(half, 1)
                attention(half + 2, par)

            attention(1, 1)
            two_experts(0, 0)
            with eng.Fori(0, E // 4 - 1) as j:
                two_experts(2 * j + 1, 1)
                two_experts(2 * j + 2, 0)
            two_experts(E // 2 - 1, 1)
            attention(S - 2, 0)
            attention(S - 1, 1)

        def value_products(eng, half, par, lg):
            at = (2 * par + lg) * GW + (QH + 1) * HD
            for t in range(S):
                i = eng.tensor_tensor(prodpv[:, lg, t, t:S], sc2[:, lg, t, t:S, :].unsqueeze(3).broadcast_to([P, S - t, QH, HD]),
                                      qkv_t[:, t, half, at:at + HD].unsqueeze(1).unsqueeze(1).broadcast_to([P, S - t, QH, HD]), ALU.mult)
            return i

        def qk_product(eng, dst, s, sp, a):
            at = slice(a * D, (a + 1) * D)
            return eng.tensor_tensor(dst.rearrange("p (h g d) -> p h g d", h=H, g=H),
                                     q_all[:, s, at].rearrange("p (h d) -> p h d", d=HD).unsqueeze(2).broadcast_to([P, H, H, HD]),
                                     k_all[:, s, at].rearrange("p (g d) -> p g d", d=HD).unsqueeze(1).broadcast_to([P, H, H, HD]), ALU.mult)

        def pv_product(eng, dst, s, sp, a):
            return eng.tensor_tensor(dst.rearrange("p (h d g) -> p h d g", h=H, g=H),
                                     score[:, sp, a * H * H:(a + 1) * H * H].rearrange("p (h g) -> p h g", g=H).unsqueeze(2)
                                     .broadcast_to([P, H, HD, H]),
                                     v_all[:, s, a * D:(a + 1) * D].rearrange("p (d g) -> p d g", g=H).unsqueeze(1)
                                     .broadcast_to([P, H, HD, H]), ALU.mult)

        @block.sync
        def _(sp):
            for s in range(S):
                sp.dma_start(xn_all[:, s], x[s].rearrange("(a p) d -> p a d", p=P)).then_inc(x_in[s // CHUNK], 16)
            for n, src in given.items():
                sp.dma_start(C[n][:], src).then_inc(W["consts_in"], 16)
            sp.wait_ge(W["zero_done"], 1)
            for k in range(CT):
                sp.dma_start(slots_d[k * E * P:(k + 1) * E * P, :].rearrange("(p a) d -> p a d", p=P),
                             zeros[:].broadcast_to([P, E, D])).then_inc(W["zero_out"], 16)

            def load(half, par):
                e = ev(half, par)
                sp.dma_start(w1_sb[:, par], w1[e]).then_inc(w_in[par], 16)
                sp.dma_start(w2_sb[:, par], w2[e].rearrange("(f p) d -> p f d", p=P)).then_inc(w_in[par], 16)
                sp.dma_start(xe[:, par], slots_d[bass.ds(e * CAP, CAP), :].rearrange("(a p) d -> p a d", p=P)).then_inc(xe_in[par], 16)

            def store(half, par):
                e = ev(half, par)
                sp.wait_ge(W["ye_done"], 3 * (e + 1))
                sp.dma_start(expert_d[bass.ds(e * CAP, CAP), :].rearrange("(a p) d -> p a d", p=P), ye[:, par]).then_inc(ye_out[par], 16)

            sp.wait_ge(W["index_done"], 1)
            sp.wait_ge(W["z2_kept"], S)
            sp.wait_ge(W["scattered"], 16 * NT * TOPK)
            load(0, 0)
            load(0, 1)
            with sp.Fori(0, E // 2 - 1) as half:
                for par in range(2):
                    store(half, par)
                    load(half + 1, par)
            store(E // 2 - 1, 0)
            store(E // 2 - 1, 1)

            def residual_in(half, par):
                sp.dma_start(xr[:, par], x[ev(half, par)].rearrange("(a p) d -> p a d", p=P)).then_inc(tail_in[par], 16)

            def result_out(half, par):
                s = ev(half, par)
                sp.wait_ge(W["res_done"], s + 1)
                sp.dma_start(out[s].rearrange("(a p) d -> p a d", p=P), xr[:, par]).then_inc(y_out[par], 16)
                sp.wait_ge(y_out[par], 16 * (half + 1))

            residual_in(0, 0)
            residual_in(0, 1)
            with sp.Fori(0, S // 2 - 1) as half:
                for par in range(2):
                    result_out(half, par)
                    residual_in(half + 1, par)
            result_out(S // 2 - 1, 0)
            result_out(S // 2 - 1, 1)

        @block.vector
        def _(dve):
            V = nc.vector
            V.memset(zeros[:], 0.0).then_inc(W["zero_done"], 1)
            V.memset(eps[:], EPS)
            V.memset(latT[LAT:LAT + 1], 1.0)
            V.memset(prodB[:], 0.0)
            V.memset(sc, NEG).then_inc(W["filled"], 1)

            count = {"moments": 0, "route": 0}

            def link(name, ins):
                ins.then_inc(W[name], 1)
                count[name] += 1
                dve.wait_ge(W[name], count[name])

            def statistics(first, last):
                with dve.Fori(first, last) as s:
                    for a in range(TT):
                        i = V.bn_stats(stat[:, s * TT + a, :], xn_all[:, s, a, :])
                    i.then_inc(W["moments"], 1)
                count["moments"] += last - first
                dve.wait_ge(W["moments"], count["moments"])

            def deviations(first, last, row, devs):
                J = slice(first * TT, last * TT)
                even, odd = stat[:, J, 1], stat[:, J, 4]
                mean, inv, dif, sq = (mom[:, r, J] for r in (row, row + 1, 4, 5))
                V.tensor_tensor(mean, even, odd, ALU.add)
                V.tensor_tensor(dif, even, odd, ALU.subtract)
                link("moments", V.tensor_tensor(sq, stat[:, J, 2], stat[:, J, 5], ALU.add))
                V.tensor_scalar(mean, mean, 0.5, None, ALU.mult)
                link("moments", V.tensor_tensor(dif, dif, dif, ALU.mult))
                V.scalar_tensor_tensor(inv, dif, float(D // 4), sq, ALU.mult, ALU.add).then_inc(W["moments"], 1)
                count["moments"] += 1
                dve.wait_ge(W["dev_done"], devs)
                link("moments", V.reciprocal(inv, inv))

            for c in range(2):
                first, last = c * CHUNK, (c + 1) * CHUNK
                dve.wait_ge(x_in[c], 16 * CHUNK)
                statistics(first, last)
                deviations(first, last, 0, 2 * c + 1)
                with dve.Fori(first, last) as s:
                    for a in range(TT):
                        i = V.tensor_scalar(xn_all[:, s, a, :], xn_all[:, s, a, :], mom[:, 0, bass.ds(s * TT + a, 1)],
                                            mom[:, 1, bass.ds(s * TT + a, 1)], ALU.subtract, ALU.mult)
                    i.then_inc(W["norm1"], 1)
                dve.wait_ge(W["norm1"], last)
                statistics(first, last)
                deviations(first, last, 2, 2 * c + 2)

            def second_norm(half, par, steady):
                s = ev(half, par)
                if steady:
                    dve.wait_ge(W["zT_ready"], s - 1)
                for a in range(TT):
                    i = V.tensor_scalar(zb[:, par, a, :], xn_all[:, s, a, :], mom[:, 2, bass.ds(s * TT + a, 1)],
                                        mom[:, 3, bass.ds(s * TT + a, 1)], ALU.subtract, ALU.mult)
                i.then_inc(W["zb_done"], 1)

            halves = lambda v: v.rearrange("p (m two f) -> p m two f", two=2, f=HD // 2)

            def keep_projections(half, par, steady):
                s = ev(half, par)
                dve.wait_ge(W["bqkv_ready"], s + 1)
                for k in range(2):
                    i = V.tensor_copy(qkv_t[:, s, 2 * k:2 * k + 2, :], bank[2 + k][:, 0:2 * QKV].rearrange("p (a c) -> p a c", a=2))
                i.then_inc(W["bqkv_done"], 1)
                dve.wait_ge(W["q_ready"], s + 1)
                wait_past(dve, "rope_q", s)
                V.tensor_tensor(t1[:, 0], bank[5][:], C["cos"][:], ALU.mult)
                V.tensor_tensor(halves(t2[:, 0])[:, :, 0, :], halves(bank[5][:])[:, :, 1, :], halves(C["sin"][:])[:, :, 0, :], ALU.mult)
                V.tensor_tensor(halves(t2[:, 0])[:, :, 1, :], halves(bank[5][:])[:, :, 0, :], halves(C["sin"][:])[:, :, 1, :],
                                ALU.mult).then_inc(W["q_read"], 1)
                dve.wait_ge(W["q_read"], s + 1)
                V.tensor_tensor(q_all[:, s, :], t1[:, 0], t2[:, 0], ALU.add).then_inc(W["rope_q"], 1)
                if steady or par:
                    rotated(half if par else half - 1, 1 - par)

            def rotated(half, par):
                s = ev(half, par)
                dve.wait_ge(W["rope_k"], s + 1)
                V.tensor_tensor(k_all[:, s, :], turned_k[par][0], turned_k[par][1], ALU.add).then_inc(W["roped_k"], 1)

            dve.wait_ge(W["consts_in"], n_consts)
            staggered(dve, second_norm, keep_projections)
            rotated(S // 2 - 1, 1)

            def unit(half, par, steady):
                u = ev(half, par)
                some = steady or par
                for lg in range(2):
                    dve.wait_ge(W["qk_prod"], 2 * u + lg + 1)
                    for t in range(S):
                        i = V.tensor_reduce(sc[:, lg, t, t:S, :], prodqk[:, lg, t, t:S, :, :], AX_X, ALU.add)
                    i.then_inc(W["qk_score"], 1)
                dve.wait_ge(W["qk_score"], 2 * u + 2)
                V.tensor_reduce(smax, sc.rearrange("p l t s q -> p l (s q) t"), AX_X, ALU.max).then_inc(W["s_max"], 1)
                dve.wait_ge(W["s_max"], u + 1)
                if some:
                    wait_past(dve, "pv_prod", u)
                V.tensor_tensor(sc2.rearrange("p l t s q -> p l t (s q)"), sc.rearrange("p l t s q -> p l t (s q)"),
                                smax.unsqueeze(2).broadcast_to([P, 2, S, S * QH]), ALU.subtract).then_inc(W["s_diff"], 1)
                if some:
                    if par:
                        block_output(half, 0)
                    else:
                        block_output(half - 1, 1)
                dve.wait_ge(W["s_exp"], u + 1)
                V.tensor_reduce(ssum, sc2.rearrange("p l t s q -> p l (s q) t"), AX_X, ALU.add).then_inc(W["s_sum"], 1)
                dve.wait_ge(W["s_sum"], u + 1)
                V.reciprocal(ssum, ssum).then_inc(W["s_rsum"], 1)
                dve.wait_ge(W["s_rsum"], u + 1)
                V.tensor_tensor(sc2.rearrange("p l t s q -> p l t (s q)"), sc2.rearrange("p l t s q -> p l t (s q)"),
                                ssum.unsqueeze(2).broadcast_to([P, 2, S, S * QH]), ALU.mult).then_inc(W["s_prob"], 1)
                dve.wait_ge(W["s_prob"], u + 1)
                value_products(V, half, par, 0).then_inc(W["pv_own"], 1)

            def block_output(half, par):
                u = ev(half, par)
                dve.wait_ge(W["pv_own"], u + 1)
                dve.wait_ge(W["pv_prod"], u + 1)
                for lg in range(2):
                    at = (2 * par + lg) * GW
                    i = V.tensor_reduce(qkv_t[:, :, half, at:at + QH * HD], prodpv[:, lg].rearrange("p t s q d -> p s (q d) t"),
                                        AX_X, ALU.add)
                i.then_inc(W["pv_sum"], 1)

            in_pairs(dve, unit)
            block_output(S // 2 - 1, 1)

            with dve.Fori(0, S // 2) as half:
                for par in range(2):
                    s = ev(half, par)
                    dve.wait_ge(W["proj_ready"], s + 1)
                    V.tensor_tensor(xn_all[:, s], bank[2 + par][:].rearrange("p (a d) -> p a d", a=TT), xn_all[:, s], ALU.add).then_inc(W["h1_done"], 1)
                    dve.wait_ge(W["h1_done"], s + 1)
                    for a in range(TT):
                        i = V.bn_stats(stat[:, s * TT + a, :], xn_all[:, s, a, :])
                    i.then_inc(W["moments"], 1)
            count["moments"] += S
            dve.wait_ge(W["moments"], count["moments"])
            deviations(0, S, 0, 5)

            def third_norm(half, par, steady):
                s = ev(half, par)
                if steady:
                    dve.wait_ge(W["z2_kept"], s - 1)
                    dve.wait_ge(W["z2T_ready"], s - 1)
                for a in range(TT):
                    i = V.tensor_scalar(zb[:, par, a, :], xn_all[:, s, a, :], mom[:, 0, bass.ds(s * TT + a, 1)],
                                        mom[:, 1, bass.ds(s * TT + a, 1)], ALU.subtract, ALU.mult)
                i.then_inc(W["z2_done"], 1)

            def keep_logits(half, par, steady):
                s = ev(half, par)
                dve.wait_ge(W["logit_ready"], s + 1)
                V.tensor_copy(logit[:].rearrange("p (s a) e -> p s (a e)", a=TT)[:, s, :], bank[6 + par][:, 0:TT * E]).then_inc(W["logit_kept"], 1)

            staggered(dve, third_norm, keep_logits)

            def step(ins):
                link("route", ins)

            lg = logit[:]
            full = lambda v: v[:].unsqueeze(2).broadcast_to([P, NT, E])
            each = lambda v: v[:].unsqueeze(1).broadcast_to([P, NT, E])
            dve.wait_ge(W["logit_kept"], S)
            for k in range(TOPK):
                step(V.tensor_reduce(best[:, k, :], lg, AX_X, ALU.max))
                step(V.tensor_tensor(tmp8[:], lg, best[:, k, :].unsqueeze(2).broadcast_to([P, NT, E]), ALU.is_equal))
                step(V.tensor_tensor(tmp8[:], tmp8[:], each(C["rev8"]), ALU.mult))
                step(V.tensor_reduce(tmp1[:], tmp8[:], AX_X, ALU.max))
                step(V.tensor_tensor(onehot[:, k], tmp8[:], full(tmp1), ALU.is_equal))
                if k == 0:
                    step(V.scalar_tensor_tensor(lg, onehot[:, 0], NEG, lg, ALU.mult, ALU.add))
            V.tensor_tensor(tmp1[:], best[:, 1, :], best[:, 0, :], ALU.subtract).then_inc(W["diff_done"], 1)
            dve.wait_ge(W["route_exp"], 1)
            step(V.tensor_scalar(tmp1[:], gate[:, 1, :], 1.0, None, ALU.add))
            step(V.reciprocal(gate[:, 0, :], tmp1[:]))
            step(V.tensor_tensor(gate[:, 1, :], gate[:, 1, :], gate[:, 0, :], ALU.mult))
            V.tensor_tensor(mask16[:], onehot[:, 0], onehot[:, 1], ALU.add).then_inc(W["mask_done"], 1)
            dve.wait_ge(W["pos_ready"], 1)
            tot = bank[1][:, 0:NT * E].rearrange("p (n e) -> p n e", e=E)
            pos = bank[0][:, 0:NT * E].rearrange("p (n e) -> p n e", e=E)
            step(V.tensor_copy(cum[:, 0], tot))
            src, sh = 0, 1
            while sh < NT:
                step(V.tensor_copy(cum[:, 1 - src, 0:sh, :], cum[:, src, 0:sh, :]))
                step(V.tensor_tensor(cum[:, 1 - src, sh:, :], cum[:, src, sh:, :], cum[:, src, 0:NT - sh, :], ALU.add))
                src, sh = 1 - src, 2 * sh
            step(V.tensor_tensor(cum[:, src], cum[:, src], tot, ALU.subtract))
            step(V.tensor_tensor(cum[:, src], cum[:, src], pos, ALU.add))
            place, fits = cum[:, src], cum[:, 1 - src]
            step(V.tensor_scalar(fits, place, float(CAP), None, ALU.is_lt))
            step(V.tensor_tensor(place, place, each(C["ebase"]), ALU.add))
            for k in range(TOPK):
                step(V.tensor_tensor(tmp8[:], onehot[:, k], fits, ALU.mult))
                step(V.tensor_reduce(fit1[:], tmp8[:], AX_X, ALU.add))
                step(V.tensor_tensor(gate[:, k, :], gate[:, k, :], fit1[:], ALU.mult))
                step(V.tensor_tensor(tmp8[:], tmp8[:], place, ALU.mult))
                step(V.tensor_reduce(tmp1[:], tmp8[:], AX_X, ALU.add))
                step(V.tensor_copy(gather_at[:, k, :], tmp1[:]))
                dmp = C["dump"][:].rearrange("p (k n) -> p k n", k=TOPK)[:, k, :]
                step(V.tensor_tensor(tmp1[:], tmp1[:], dmp, ALU.add))
                step(V.tensor_tensor(fit1[:], fit1[:], dmp, ALU.mult))
                step(V.tensor_tensor(tmp1[:], tmp1[:], fit1[:], ALU.subtract))
                step(V.tensor_copy(scatter_at[:, k, :], tmp1[:]))
            V.tensor_copy(fit1[:], tmp1[:]).then_inc(W["index_done"], 1)

            def multiply_add(done, call, s, sp, helped, kind):
                own = TT - 1 if helped else TT
                def total(a):
                    src = prodA[:, a % 2, :] if a < own else prodB[:, 0 if kind == "qk" else 1, :]
                    if a < own:
                        dve.wait_ge(W["prod_done"], done + a + 1)
                    else:
                        dve.wait_ge(W["help_qk" if kind == "qk" else "help_pv"], s - HELPED + 1)
                    if kind == "qk":
                        return V.tensor_reduce(score[:, sp, a * H * H:(a + 1) * H * H], src.rearrange("p (m d) -> p m d", d=HD), AX_X, ALU.add)
                    return V.tensor_reduce(ao[:, sp, a, :], src.rearrange("p (m g) -> p m g", g=H), AX_X, ALU.add)
                mult = qk_product if kind == "qk" else pv_product
                if not isinstance(call, int) or call > 0:
                    dve.wait_ge(W["sum_done"], (TT - 1) * call)
                for a in range(own):
                    if a >= 2:
                        total(a - 2).then_inc(W["sum_done"], 1)
                        dve.wait_ge(W["sum_done"], (TT - 1) * call + a - 1)
                    mult(V, prodA[:, a % 2, :], s, sp, a).then_inc(W["prod_done"], 1)
                for a in range(own - 2, TT - 1):
                    total(a).then_inc(W["sum_done"], 1)
                total(TT - 1).then_inc(W["score_done" if kind == "qk" else "out_sum"], 1)

            rows = lambda v: v.rearrange("p (m g) -> p m g", g=H)
            over = lambda v: v.unsqueeze(2).broadcast_to([P, TT * H, H])

            def batch(half, par, s, done, helped, more, more_helped):
                dve.wait_ge(W["score_done"], s + 1)
                V.tensor_reduce(hmax[:, par, :], rows(score[:, par]), AX_X, ALU.max).then_inc(W["row_max"], 1)
                dve.wait_ge(W["row_max"], s + 1)
                V.tensor_tensor(rows(score[:, par]), rows(score[:, par]), over(hmax[:, par, :]), ALU.subtract).then_inc(W["row_diff"], 1)
                if more:
                    if not isinstance(s, int) or s >= 1:
                        wait_past(dve, "out_sum", s)
                    multiply_add(done, 2 * s + 1, s + 1, 1 - par, more_helped, "qk")
                    done = done + (TT - 1 if more_helped else TT)
                if not isinstance(s, int) or s >= 1:
                    wait_past(dve, "attn_ready", s)
                    V.tensor_tensor(q_all[:, s - 1, :].rearrange("p (a d) -> p a d", a=TT), bank[7][:].rearrange("p (a d) -> p a d", a=TT),
                                    C["bout"][:].unsqueeze(1).broadcast_to([P, TT, D]), ALU.add).then_inc(W["attn_done"], 1)
                dve.wait_ge(W["row_exp"], s + 1)
                V.tensor_reduce(hsum[:, par, :], rows(score[:, par]), AX_X, ALU.add).then_inc(W["row_sum"], 1)
                dve.wait_ge(W["row_sum"], s + 1)
                V.reciprocal(hsum[:, par, :], hsum[:, par, :]).then_inc(W["row_inv"], 1)
                dve.wait_ge(W["row_inv"], s + 1)
                if not isinstance(s, int) or s >= 2:
                    dve.wait_ge(W["ao_ready"], s - 1)
                if more:
                    dve.wait_ge(W["score_done"], s + 2)
                multiply_add(done, 2 * s + 2 if more else 2 * S - 1, s, par, helped, "pv")
                dve.wait_ge(W["out_sum"], s + 1)
                o = ao[:, par].rearrange("p a (h d) -> p (a h) d", d=HD)
                V.tensor_tensor(o, o, hsum[:, par, :].unsqueeze(2).broadcast_to([P, TT * H, HD]), ALU.mult).then_inc(W["ao_done"], 1)

            dve.wait_ge(W["roped_k"], S)
            dve.wait_ge(W["v_done"], S)
            multiply_add(0, 0, 0, 0, False, "qk")
            batch(0, 0, 0, 4, False, True, False)
            batch(0, 1, 1, 12, False, True, True)
            with dve.Fori(1, S // 2 - 1) as half:
                for par in range(2):
                    s = ev(half, par)
                    batch(half, par, s, 6 * s + 7, True, True, True)
            batch(S // 2 - 1, 0, S - 2, 6 * (S - 2) + 7, True, True, True)
            batch(S // 2 - 1, 1, S - 1, 6 * (S - 1) + 7, True, False, False)
            dve.wait_ge(W["attn_ready"], S)
            V.tensor_tensor(q_all[:, S - 1, :].rearrange("p (a d) -> p a d", a=TT), bank[7][:].rearrange("p (a d) -> p a d", a=TT),
                            C["bout"][:].unsqueeze(1).broadcast_to([P, TT, D]), ALU.add).then_inc(W["attn_done"], 1)
            dve.wait_ge(W["attn_done"], S)

            with dve.Fori(0, S // 2) as half:
                for par in range(2):
                    s = ev(half, par)
                    V.tensor_copy(gate_s[:, par], gate[:].rearrange("p k (s a) -> p k s a", a=TT)[:, :, s, :]).then_inc(W["gate_in"], 1)
                    dve.wait_ge(W["gate_in"], s + 1)
                    dve.wait_ge(gathered[par], 16 * TT * TOPK * (half + 1))
                    for a in range(TT):
                        i = V.scalar_tensor_tensor(fb[:, par, a, :], yg[:, par, a, 0, :], gate_s[:, par, 0, a:a + 1], xn_all[:, s, a, :], ALU.mult, ALU.add)
                    i.then_inc(W["f_step"], 1)
                    dve.wait_ge(W["f_step"], s + 1)
                    for a in range(TT):
                        i = V.scalar_tensor_tensor(fb[:, par, a, :], yg[:, par, a, 1, :], gate_s[:, par, 1, a:a + 1], fb[:, par, a, :], ALU.mult, ALU.add)
                    i.then_inc(W["f_done"], 1)
                    dve.wait_ge(W["silu_done"], s + 1)
                    V.tensor_tensor(gb[:, par].rearrange("p a d -> p (a d)"), gb[:, par].rearrange("p a d -> p (a d)"), q_all[:, s, :], ALU.mult).then_inc(W["gate_done"], 1)
                    dve.wait_ge(W["gate_done"], s + 1)
                    dve.wait_ge(tail_in[par], 16 * (half + 1))
                    V.tensor_tensor(xr[:, par], xr[:, par], gb[:, par], ALU.add).then_inc(W["res_done"], 1)

        @block.tensor
        def _(pe):
            M = nc.tensor
            pe.wait_ge(W["consts_in"], n_consts)
            pe.wait_ge(W["filled"], 1)

            def transposes(dst, src):
                for a in range(TT):
                    i = M.transpose(dst[:, a * P:(a + 1) * P], src[:, a, :], C["identf"][:])
                return i

            def projected(dst, src, weight, width=D, stop=True):
                for a in range(TT):
                    i = M.matmul(dst[:, a * width:(a + 1) * width], src[:, a * P:(a + 1) * P], weight[:], start=True, stop=stop)
                return i

            def turn(half, par, steady):
                s = ev(half, par)
                pe.wait_ge(W["xnb_done"], s + 1)
                wait_past(pe, "xnT_done", s)
                transposes(bank[0], xnb[:, par]).then_inc(W["xnT_ready"], 1)
                pe.wait_ge(W["zb_done"], s + 1)
                wait_past(pe, "lnT_done", s)
                transposes(bank[1], zb[:, par]).then_inc(W["zT_ready"], 1)

            def project(half, par, steady):
                s = ev(half, par)
                pe.wait_ge(W["xnT_done"], s + 1)
                wait_past(pe, "lat_done", s)
                M.matmul(bank[4][0:LAT, :], C["wdown"][:], xnT[:, par, :], start=True, stop=True).then_inc(W["lat_ready"], 1)
                wait_past(pe, "q_read", s)
                for a in range(TT):
                    dst = bank[5][:, a * D:(a + 1) * D]
                    M.matmul(dst, xnT[:, par, a * P:(a + 1) * P], C["wq"][:], start=True, stop=False)
                    i = M.matmul(dst, C["ones1"][:], C["bq"][:], start=False, stop=True)
                i.then_inc(W["q_ready"], 1)
                pe.wait_ge(W["lnT_done"], s + 1)
                wait_past(pe, "bqkv_done", s)
                for a in range(TT):
                    i = M.matmul(bank[2 + a // 2][:, (a % 2) * QKV:(a % 2 + 1) * QKV], lnT[:, par, a * P:(a + 1) * P], C["wqkv"][:], start=True, stop=True)
                i.then_inc(W["bqkv_ready"], 1)
                pe.wait_ge(W["lat_done"], s + 1)
                wait_past(pe, "k_done", s)
                projected(bank[6], latT[0:LAT + 1, par, :], C["wupk"]).then_inc(W["k_ready"], 1)
                wait_past(pe, "v_done", s)
                projected(bank[7], latT[0:LAT + 1, par, :], C["wupv"]).then_inc(W["v_ready"], 1)

            staggered(pe, turn, project)
            pe.wait_ge(W["bqkv_done"], S)
            pe.wait_ge(W["xnT_done"], S)

            def turn_block(half, par, steady):
                s = ev(half, par)
                pe.wait_ge(W["aoc_done"], s + 1)
                if steady:
                    pe.wait_ge(W["bT_done"], s - 1)
                transposes(bank[par], aoc[:, par]).then_inc(W["bT_ready"], 1)

            def project_block(half, par, steady):
                s = ev(half, par)
                pe.wait_ge(W["bT_done"], s + 1)
                if steady:
                    pe.wait_ge(W["h1_done"], s - 1)
                projected(bank[2 + par], bT, C["wproj"]).then_inc(W["proj_ready"], 1)

            staggered(pe, turn_block, project_block)
            pe.wait_ge(W["v_done"], S)
            pe.wait_ge(W["k_done"], S)

            def turn_normed(half, par, steady):
                s = ev(half, par)
                pe.wait_ge(W["z2_done"], s + 1)
                if steady:
                    pe.wait_ge(W["x2T_done"], s - 1)
                transposes(bank[4 + par], zb[:, par]).then_inc(W["z2T_ready"], 1)

            def router(half, par, steady):
                s = ev(half, par)
                pe.wait_ge(W["x2T_done"], s + 1)
                if steady:
                    pe.wait_ge(W["logit_kept"], s - 1)
                projected(bank[6 + par], lnT[:, par, :], C["wrouter"], E).then_inc(W["logit_ready"], 1)

            staggered(pe, turn_normed, router)
            pe.wait_ge(W["mask_done"], 1)
            mask = mask16[:].rearrange("p n e -> p (n e)")
            M.matmul(bank[0][:, 0:NT * E], C["tri"][:], mask, start=True, stop=True)
            M.matmul(bank[1][:, 0:NT * E], C["allones"][:], mask, start=True, stop=True).then_inc(W["pos_ready"], 1)
            pe.wait_ge(W["index_done"], 1)

            def expert(half, par):
                e = ev(half, par)
                pe.wait_ge(xe_in[par], 16 * (half + 1))
                pe.wait_ge(w_in[par], 32 * (half + 1))
                wait_past(pe, "gelu_done", 6 * e)
                for q in range(3):
                    for a in range(4 * q, min(4 * q + 4, CT)):
                        i = M.transpose(bank[q][:, (a % 4) * P:(a % 4 + 1) * P], xe[:, par, a, :], C["identf"][:])
                    i.then_inc(W["xeT_ready"], 1)
                wait_past(pe, "ye_done", 3 * e)
                for f in range(FH):
                    for m, (at, n) in enumerate(chunks):
                        k = 3 * f + m
                        pe.wait_ge(W["xeT_done"], 3 * e + m + 1)
                        M.matmul(bank[(3 + k) % 6][:, 0:n], w1_sb[:, par, f * P:(f + 1) * P], xeT[:, at:at + n],
                                 start=True, stop=True).then_inc(W["fc1_ready"], 1)
                pe.wait_ge(W["gelu_done"], 6 * e + 6)
                for q in range(3):
                    for a in range(4 * q, min(4 * q + 4, CT)):
                        for f in range(FH):
                            i = M.matmul(bank[3 + q][:, (a % 4) * P:(a % 4 + 1) * P], hT[:, f, a * P:(a + 1) * P],
                                         w2_sb[:, par, f, :], start=(f == 0), stop=(f == FH - 1))
                    i.then_inc(W["fc2_ready"], 1)

            def attention_out(s, par):
                pe.wait_ge(W["ao_done"], s + 1)
                wait_past(pe, "aoT_done", s)
                transposes(bank[6], ao[:, par]).then_inc(W["ao_ready"], 1)
                pe.wait_ge(W["aoT_done"], s + 1)
                wait_past(pe, "attn_done", s)
                projected(bank[7], aoT, C["wout"]).then_inc(W["attn_ready"], 1)

            fourth(pe, expert, lambda s, par: attention_out(s - 1, 1 - par))
            attention_out(S - 1, 1)

        @block.scalar
        def _(act):
            A = nc.scalar

            def deviation(first, last, row, links):
                act.wait_ge(W["moments"], links)
                v = mom[:, row + 1, first * TT:last * TT]
                A.activation(v, v, ACT.Sqrt, bias=eps[:], scale=1.0 / D).then_inc(W["dev_done"], 1)

            act.wait_ge(W["filled"], 1)
            n = 0
            for c in range(2):
                for row in (0, 2):
                    deviation(c * CHUNK, (c + 1) * CHUNK, row, n + CHUNK + 3)
                    n += CHUNK + 4
            act.wait_ge(W["consts_in"], n_consts)

            def copy_normed(half, par, steady):
                s = ev(half, par)
                if steady:
                    act.wait_ge(W["xnT_ready"], s - 1)
                A.copy(xnb[:, par], xn_all[:, s]).then_inc(W["xnb_done"], 1)

            def keep(half, par, steady):
                s = ev(half, par)
                if steady:
                    act.wait_ge(W["q_ready"], s - 1)
                act.wait_ge(W["xnT_ready"], s + 1)
                A.copy(xnT[:, par, :], bank[0][:]).then_inc(W["xnT_done"], 1)
                if steady:
                    act.wait_ge(W["bqkv_ready"], s - 1)
                    act.wait_ge(W["v_ready"], s - 1)
                act.wait_ge(W["zT_ready"], s + 1)
                A.activation(lnT[:, par, :], bank[1][:], ACT.Identity, bias=C["ln1b"][:], scale=C["ln1w"][:]).then_inc(W["lnT_done"], 1)
                act.wait_ge(W["lat_ready"], s + 1)
                A.activation(latT[0:LAT, par, :], bank[4][0:LAT, :], ACT.Identity, bias=C["bdown"][:]).then_inc(W["lat_done"], 1)
                act.wait_ge(W["k_ready"], s + 1)
                A.copy(k_all[:, s, :], bank[6][:]).then_inc(W["k_done"], 1)
                act.wait_ge(W["v_ready"], s + 1)
                A.copy(v_all[:, s, :], bank[7][:]).then_inc(W["v_done"], 1)

            act.wait_ge(W["norm1"], S)
            staggered(act, copy_normed, keep)

            with act.Fori(0, S) as u:
                act.wait_ge(W["s_diff"], u + 1)
                A.activation(sc2, sc2, ACT.Exp, scale=SCALE).then_inc(W["s_exp"], 1)

            def copy_block(half, par, steady):
                s = ev(half, par)
                if steady:
                    act.wait_ge(W["bT_ready"], s - 1)
                A.copy(aoc[:, par].rearrange("p a (g w) -> p a g w", g=G),
                       qkv_t[:, s].rearrange("p a (g w) -> p a g w", g=G)[:, :, :, 0:QH * HD]).then_inc(W["aoc_done"], 1)

            def keep_block(half, par, steady):
                s = ev(half, par)
                act.wait_ge(W["bT_ready"], s + 1)
                wait_past(act, "proj_ready", s)
                A.copy(bT, bank[par][:]).then_inc(W["bT_done"], 1)

            act.wait_ge(W["pv_sum"], S)
            staggered(act, copy_block, keep_block)
            deviation(0, S, 0, n + S + 3)

            def keep_rows(half, par, steady):
                s = ev(half, par)
                act.wait_ge(W["z2_done"], s + 1)
                A.copy(z2_all[:, s], zb[:, par]).then_inc(W["z2_kept"], 1)

            def keep_turned(half, par, steady):
                s = ev(half, par)
                act.wait_ge(W["z2T_ready"], s + 1)
                if steady:
                    act.wait_ge(W["logit_ready"], s - 1)
                A.activation(lnT[:, par, :], bank[4 + par][:], ACT.Identity, bias=C["ln2b"][:], scale=C["ln2w"][:]).then_inc(W["x2T_done"], 1)

            act.wait_ge(W["aoc_done"], S)
            staggered(act, keep_rows, keep_turned)
            act.wait_ge(W["diff_done"], 1)
            A.activation(gate[:, 1, :], tmp1[:], ACT.Exp).then_inc(W["route_exp"], 1)
            act.wait_ge(W["index_done"], 1)

            def expert(half, par):
                e = ev(half, par)
                wait_past(act, "fc1_ready", 6 * e)
                for m, (at, n) in enumerate(chunks):
                    act.wait_ge(W["xeT_ready"], 3 * e + m + 1)
                    A.activation(xeT[:, at:at + n], bank[m][:, 0:n], ACT.Identity, bias=C["ln2b"][:], scale=C["ln2w"][:]).then_inc(W["xeT_done"], 1)
                wait_past(act, "fc2_ready", 3 * e)
                for f in range(FH):
                    for m, (at, n) in enumerate(chunks):
                        k = 3 * f + m
                        act.wait_ge(W["fc1_ready"], 6 * e + k + 1)
                        A.activation(hT[:, f, at:at + n], bank[(3 + k) % 6][:, 0:n], ACT.Gelu_apprx_tanh).then_inc(W["gelu_done"], 1)
                wait_past(act, ye_out[par], 16 * half)
                for q in range(3):
                    n = min(4, CT - 4 * q)
                    act.wait_ge(W["fc2_ready"], 3 * e + q + 1)
                    A.copy(ye[:, par, 4 * q:4 * q + n, :], bank[3 + q][:, 0:n * D].rearrange("p (a d) -> p a d", d=D)).then_inc(W["ye_done"], 1)

            def exponentials(s, par):
                act.wait_ge(W["row_diff"], s + 1)
                A.activation(score[:, par, :], score[:, par, :], ACT.Exp, scale=SCALE).then_inc(W["row_exp"], 1)

            def keep_attention(s):
                act.wait_ge(W["ao_ready"], s + 1)
                wait_past(act, "attn_ready", s)
                A.copy(aoT[:], bank[6][:]).then_inc(W["aoT_done"], 1)

            def attention(s, par):
                exponentials(s, par)
                keep_attention(s - 1)

            exponentials(0, 0)
            fourth(act, expert, attention)
            keep_attention(S - 1)

            def silu(half, par, steady):
                s = ev(half, par)
                act.wait_ge(W["f_done"], s + 1)
                if steady:
                    act.wait_ge(W["gate_done"], s - 1)
                A.activation(gb[:, par], fb[:, par], ACT.Silu).then_inc(W["silu_done"], 1)

            in_pairs(act, silu)

        @block.gpsimd
        def _(pool):
            Q = nc.gpsimd
            halves = lambda v: v.rearrange("p (m two f) -> p m two f", two=2, f=HD // 2)
            pool.wait_ge(W["consts_in"], n_consts)
            def rotate(half, par, steady):
                s = ev(half, par)
                k, (with_cos, with_sin) = k_all[:, s, :], turned_k[par]
                if steady:
                    pool.wait_ge(W["roped_k"], s - 1)
                pool.wait_ge(W["k_done"], s + 1)
                Q.tensor_tensor(with_cos, k, C["cos"][:], ALU.mult)
                Q.tensor_tensor(halves(with_sin)[:, :, 0, :], halves(k)[:, :, 1, :], halves(C["sin"][:])[:, :, 0, :], ALU.mult)
                Q.tensor_tensor(halves(with_sin)[:, :, 1, :], halves(k)[:, :, 0, :], halves(C["sin"][:])[:, :, 1, :],
                                ALU.mult).then_inc(W["rope_k"], 1)

            in_pairs(pool, rotate)

            def key_products(half, par):
                u = ev(half, par)
                for lg in range(2):
                    at = (2 * par + lg) * GW
                    if not isinstance(u, int) or u > 0:
                        pool.wait_ge(W["qk_score"], 2 * u - 1 + lg)
                    for t in range(S):
                        i = Q.tensor_tensor(prodqk[:, lg, t, t:S], qkv_t[:, t:S, half, at:at + QH * HD].rearrange("p s (q d) -> p s q d", d=HD),
                                            qkv_t[:, t, half, at + QH * HD:at + (QH + 1) * HD].unsqueeze(1).unsqueeze(1)
                                            .broadcast_to([P, S - t, QH, HD]), ALU.mult)
                    i.then_inc(W["qk_prod"], 1)

            def own_values(half, par):
                u = ev(half, par)
                pool.wait_ge(W["s_prob"], u + 1)
                value_products(Q, half, par, 1).then_inc(W["pv_prod"], 1)

            pool.wait_ge(W["bqkv_done"], S)
            pool.wait_ge(W["filled"], 1)
            key_products(0, 0)
            key_products(0, 1)
            own_values(0, 0)
            with pool.Fori(1, S // 2) as half:
                key_products(half, 0)
                own_values(half - 1, 1)
                key_products(half, 1)
                own_values(half, 0)
            own_values(S // 2 - 1, 1)

            def help_scores(s, par):
                wait_past(pool, "score_done", s)
                qk_product(Q, prodB[:, 0, :], s, par, TT - 1).then_inc(W["help_qk"], 1)

            def help_values(s, par):
                pool.wait_ge(W["row_exp"], s + 1)
                wait_past(pool, "out_sum", s)
                pv_product(Q, prodB[:, 1, :], s, par, TT - 1).then_inc(W["help_pv"], 1)

            pool.wait_ge(W["pv_sum"], S)
            pool.wait_ge(W["rope_q"], S)
            pool.wait_ge(W["v_done"], S)

            pool.wait_ge(W["zero_out"], 16 * CT)
            pool.wait_ge(W["index_done"], 1)
            pool.wait_ge(W["z2_kept"], S)
            for k in range(TOPK):
                for n in range(NT):
                    Q.indirect_dma_start(slots_d, bass.IndirectOffsetOnAxis(ap=scatter_at[:, k, n:n + 1], axis=0),
                                         z2_all[:, n // TT, n % TT, :], None).then_inc(W["scattered"], 16)
            help_scores(HELPED, 0)
            with pool.Fori(1, S // 2 - 1) as half:
                for par in range(2):
                    help_scores(ev(half, par) + 1, 1 - par)
                    help_values(ev(half, par), par)
            help_scores(S - 1, 1)
            help_values(S - 2, 0)
            help_values(S - 1, 1)

            for par in range(2):
                pool.wait_ge(ye_out[par], 16 * (E // 2))
            for s in range(S):
                if s >= 2:
                    pool.wait_ge(W["f_done"], s - 1)
                for a in range(TT):
                    for k in range(TOPK):
                        n = s * TT + a
                        Q.indirect_dma_start(yg[:, s % 2, a, k, :], None, expert_d,
                                             bass.IndirectOffsetOnAxis(ap=gather_at[:, k, n:n + 1], axis=0)).then_inc(gathered[s % 2], 16)


def kernel(L0_attn_x, L0_attn_Wq, L0_attn_bq, L0_attn_Wdown, L0_attn_bdown, L0_attn_Wup, L0_attn_bup, L0_attn_Wout,
           L0_attn_bout, L0_ffn_ln1_weight, L0_ffn_ln1_bias, L0_ffn_ln2_weight, L0_ffn_ln2_bias, L0_ffn_qkv_weight,
           L0_ffn_proj_weight, L0_ffn_router_weight, L0_ffn_moe_w1, L0_ffn_moe_w2):
    import concourse.bacc as bacc
    import ml_dtypes
    from concourse.bass_utils import run_bass_kernel_spmd

    wup = np.concatenate([np.asarray(L0_attn_Wup), np.asarray(L0_attn_bup)[None]]).reshape(LAT + 1, H, 2, HD)
    col = lambda v: np.asarray(v).reshape(-1, 1)
    own = np.ascontiguousarray

    freq = (1.0 / 10000.0 ** (np.arange(0, HD, 2, dtype=np.float32) / np.float32(HD))).astype(np.float32)
    angle = (np.arange(T, dtype=np.float32)[:, None] * freq).reshape(TT, P, 1, 1, HD // 2).transpose(1, 0, 2, 3, 4)
    table = lambda first, second: own(np.broadcast_to(np.concatenate([first, second], 3), (P, TT, H, 2, HD // 2)), np.float32).reshape(P, TT * D)
    bf16 = ml_dtypes.bfloat16
    token = np.arange(NT)[None, None, :] * P + np.arange(P)[:, None, None]
    arrays = dict(
        x=np.asarray(L0_attn_x), wq=np.asarray(L0_attn_Wq), bq=np.asarray(L0_attn_bq)[None], wdown=np.asarray(L0_attn_Wdown),
        bdown=col(L0_attn_bdown), wupk=own(wup[:, :, 0].reshape(LAT + 1, D)), wupv=own(wup[:, :, 1].transpose(0, 2, 1)).reshape(LAT + 1, D),
        wout=np.asarray(L0_attn_Wout), bout=np.asarray(L0_attn_bout),
        ln1w=col(L0_ffn_ln1_weight), ln1b=col(L0_ffn_ln1_bias), ln2w=col(L0_ffn_ln2_weight), ln2b=col(L0_ffn_ln2_bias),
        wqkv=own(np.asarray(L0_ffn_qkv_weight).T), wproj=own(np.asarray(L0_ffn_proj_weight).T),
        wrouter=np.asarray(L0_ffn_router_weight), w1=np.asarray(L0_ffn_moe_w1), w2=np.asarray(L0_ffn_moe_w2),
        cos=table(np.cos(angle), np.cos(angle)), sin=table(-np.sin(angle), np.sin(angle)),
        identf=np.eye(P, dtype=np.float32), ones1=np.ones((1, P), np.float32),
        tri=np.triu(np.ones((P, P), np.float32), 1).astype(bf16), allones=np.ones((P, P), bf16),
        rev8=np.tile(np.arange(E, 0, -1, dtype=np.float32), (P, 1)),
        ebase=np.tile(np.arange(E, dtype=np.float32) * CAP, (P, 1)),
        dump=(SLOTS + TOPK * token + np.arange(TOPK)[None, :, None]).reshape(P, -1).astype(np.float32),
    )
    nc = bacc.Bacc("TRN2", target_bir_lowering=False, num_devices=1)
    aps = {n: nc.dram_tensor(f"in_{n}", a.shape, mybir.dt.from_np(a.dtype), kind="ExternalInput").ap() for n, a in arrays.items()}
    out = nc.dram_tensor("out", (S, T, D), F32, kind="ExternalOutput").ap()
    build(nc, **aps, out=out)
    r = run_bass_kernel_spmd(nc, [{f"in_{n}": a for n, a in arrays.items()}], core_ids=[0])
    return r.results[0]["out"]
```

```python
from contextlib import ExitStack

import numpy as np

import concourse.bass as bass
from concourse import mybir

F32 = mybir.dt.float32
BF16 = mybir.dt.bfloat16
U32 = mybir.dt.uint32
ALU = mybir.AluOpType
ACT = mybir.ActivationFunctionType
AX_X = mybir.AxisListType.X

P = 128
S, T, D = 8, 512, 128
TT = T // P
NT = S * TT
H, HD = 16, 8
LAT = 32
G, QH = 4, 4
GW = (QH + 2) * HD
QKV = G * GW
E, FF, TOPK = 8, 256, 2
FH = FF // P
CAP = int(np.ceil(S * T * TOPK / E * 1.25))
CT = CAP // P
SLOTS = E * CAP
EPS = 1e-5
SCALE = float(1.0 / np.sqrt(np.float32(HD)))
NEG = -3.0e38
CHUNK = S // 2
LOOP = range(3, 7)
HELPED_QK = [2, 1, 0] + [2] * len(LOOP) + [0]
HELPED_PV = range(2, 6)
SUMMED_QK, QK_TILES = (0, 1, 2, 7), 2
BUSY, FEW_TILES = range(2, 6), 2
BANKS = 4


def build(nc, x, wq, bq, wdown, bdown, wupk, wupv, wout, bout, ln1w, ln1b, ln2w, ln2b,
          wqkv, wproj, wrouter, w1, w2, cos, sin, identf, ones1, tri, allones, rev8, ebase, dump, out):
    slots_d = nc.dram_tensor("slot_rows", (SLOTS + S * T * TOPK, D), F32, kind="Internal").ap()
    expert_d = nc.dram_tensor("expert_rows", (SLOTS, D), F32, kind="Internal").ap()

    with ExitStack() as ctx:
        def sb(name, shape, dt=F32):
            return ctx.enter_context(nc.sbuf_tensor(name, shape, dt))

        def ps(name, shape, dt=F32):
            return ctx.enter_context(nc.psum_tensor(name, shape, dt))

        def sem(name):
            return ctx.enter_context(nc.semaphore(name))

        def room(of, at, *shape):
            n = int(np.prod(shape))
            names = [f"a{k}" for k in range(len(shape))]
            return of[:, at:at + n].rearrange(f"p ({' '.join(names)}) -> p {' '.join(names)}", **dict(zip(names, shape)))

        given = dict(identf=identf, ln1w=ln1w, ln1b=ln1b, wqkv=wqkv, wdown=wdown, bdown=bdown, wq=wq, bq=bq, ones1=ones1,
                     wupk=wupk, wupv=wupv, cos=cos, sin=sin, wproj=wproj, ln2w=ln2w, ln2b=ln2b, wrouter=wrouter,
                     wout=wout, bout=bout.partition_broadcast(P), rev8=rev8, ebase=ebase, dump=dump, tri=tri, allones=allones)
        sizes = dict(identf=[P, P], ln1w=[P, 1], ln1b=[P, 1], wqkv=[P, QKV], wdown=[P, LAT], bdown=[LAT, 1], wq=[P, D], bq=[1, D],
                     ones1=[1, P], wupk=[LAT + 1, D], wupv=[LAT + 1, D], cos=[P, TT * D], sin=[P, TT * D], wproj=[P, D],
                     ln2w=[P, 1], ln2b=[P, 1], wrouter=[P, E], wout=[P, D], bout=[P, D], rev8=[P, E], ebase=[P, E],
                     dump=[P, TOPK * NT], tri=[P, P], allones=[P, P])
        C = {n: sb("c_" + n, sizes[n], BF16 if n in ("tri", "allones") else F32) for n in given}

        xn_all = sb("xn_all", [P, S, TT, D])
        qkv_all = sb("qkv_all", [P, S, TT * QKV])
        qkv_t = qkv_all[:].rearrange("p s (a c) -> p s a c", a=TT)
        z2_all = qkv_all[:, :, 0:TT * D].rearrange("p s (a d) -> p s a d", a=TT)
        q_all = sb("q_all", [P, S, TT * D])
        k_all = sb("k_all", [P, S, TT * D])
        v_all = sb("v_all", [P, S, TT * D])
        prod = sb("prod", [P, 6 * H * H * HD])
        prodA, prodB, prodC = (room(prod, i * 2 * H * H * HD, 2, H * H * HD) for i in range(3))
        score = sb("score", [P, 2, TT * H * H])
        hmax = sb("hmax", [P, 2, TT * H])
        hsum = sb("hsum", [P, 2, TT * H])
        ao = sb("ao", [P, 2, TT, D])
        stat = sb("stat", [P, NT, 6])
        mom = sb("mom", [P, 6, NT])
        eps = sb("eps", [P, 1])
        zeros = sb("zeros", [P, 1, D])

        flat = sb("flat", [P, 8 * CAP])
        zb = room(flat, 0, CHUNK, TT, D)
        xnb = room(flat, 0, 2, TT, D)
        xnT = room(flat, 2048, 2, T)
        lnT = room(flat, 3072, 2, T)
        latT = room(flat, 4096, 2, T)
        aoc = room(flat, 5120, 2, TT, D)
        bT = room(flat, 6144, T)
        t1 = room(flat, 6656, 2, TT * D)
        t2 = room(flat, 7680, 2, TT * D)
        t3 = room(flat, 8704, 2, TT * D)
        turned_k = ((t1[:, 1], t2[:, 1]), (t3[:, 0], t3[:, 1]))
        xe = room(flat, 0, 2, CT, D)
        xeT = room(flat, 2 * CAP, CAP)
        hT = room(flat, 3 * CAP, FH, CAP)
        ye = room(flat, 5 * CAP, 2, CT, D)
        w1_sb = room(flat, 7 * CAP, 2, FF)
        w2_sb = room(flat, 7 * CAP + 2 * FF, 2, FH, D)
        value_buf = [prodB[:, 0, :], prodB[:, 1, :], prodC[:, 0, :], prodC[:, 1, :]]
        past = room(qkv_all[:].rearrange("p s c -> p (s c)"), 0, 2, H * H * HD)
        help_buf = {0: {2: value_buf[0], 3: value_buf[1]}, 1: {3: value_buf[2]}}
        help_buf.update({s: {2: past[:, 0], 3: past[:, 1]} for s in range(2, S)})
        yg = room(flat, 0, S, TT, TOPK, D)
        gb = room(flat, 9216, 2, TT, D)
        xr = prodA.rearrange("p l (s a d) -> p (l s) a d", a=TT, d=D)
        aoT = sb("aoT", [P, T])

        UNIT = S * (S + 1) // 2 * QH * HD

        def from_key(kind, par, t):
            first = (t * S - t * (t - 1) // 2) * QH * HD
            return room(prod, (2 * kind + par) * 2 * UNIT, 2, UNIT)[:, :, first:first + (S - t) * QH * HD]
        sc = score[:, 0, 0:2 * S * S * QH].rearrange("p (l t s q) -> p l t s q", l=2, t=S, s=S)
        sc2 = score[:, 0, 2 * S * S * QH:].rearrange("p (l t s q) -> p l t s q", l=2, t=S, s=S)
        smax = hmax[:, 0, :].rearrange("p (l m) -> p l m", l=2)
        ssum = hsum[:, 0, :].rearrange("p (l m) -> p l m", l=2)

        logit = sb("logit", [P, NT, E])
        best = sb("best", [P, TOPK, NT])
        onehot = room(prodC[:, 1, :], 3 * NT * E, TOPK, NT, E)
        cum = room(prodC[:, 1, :], 0, 2, NT, E)
        tmp8 = room(prodC[:, 1, :], 2 * NT * E, NT, E)
        tmp1 = sb("tmp1", [P, NT])
        fit1 = sb("fit1", [P, NT])
        gate = sb("gate", [P, TOPK, NT])
        gate_s = sb("gate_s", [P, 2, TOPK, TT])
        mask16 = sb("mask16", [P, NT, E], BF16)
        gather_at = sb("gather_at", [P, TOPK, NT], U32)
        scatter_at = sb("scatter_at", [P, TOPK, NT], U32)

        bank = [ps(f"bank{i}", [P, T]) for i in range(8)]

        names = """consts_in filled
            moments norm1 norm2 dev_done xnb_done zb_done xnT_ready xnT_done zT_ready lnT_done lat_ready lat_done
            bqkv_ready bqkv_done q_ready q_read k_ready k_done v_ready v_done q_done rope_q rope_k roped_k
            qk_prod qk_score s_max s_diff s_exp s_sum s_rsum s_prob pv_own pv_prod pv_ready block_kept
            aoc_done bT_ready bT_done proj_ready h1_done z2_done z2_kept z2T_ready x2T_done logit_ready logit_kept
            route diff_done route_exp mask_done pos_ready index_done zero_done zero_out scattered
            prod_done sum_done help_qk help_pv score_done row_max row_diff row_exp row_sum row_inv score_sum value_prod value_part value_sum ao_done ao_ready aoT_done
            attn_ready attn_done
            part_ready part_kept
            tail_in gate_in f_step silu_done gate_done res_done""".split()
        W = {n: sem(n) for n in names}
        x_in, w_in, xe_in, ye_out, gathered, y_out = ([sem(f"{n}{i}") for i in range(2)] for n in (
            "x_in", "w_in", "xe_in", "ye_out", "gathered", "y_out"))
        block = ctx.enter_context(nc.Block())

        def ev(half, par):
            return 2 * half + par

        def after(half, par):
            return (half, 1) if par == 0 else (half + 1, 0)

        def wait_past(eng, name, count):
            if not isinstance(count, int) or count > 0:
                eng.wait_ge(W[name] if isinstance(name, str) else name, count)

        def staggered(eng, first, second):
            first(0, 0, False)
            first(0, 1, False)
            second(0, 0, False)
            first(1, 0, True)
            second(0, 1, False)
            with eng.Fori(1, S // 2 - 1) as half:
                for par in range(2):
                    first(*after(half, par), True)
                    second(half, par, True)
            first(S // 2 - 1, 1, True)
            second(S // 2 - 1, 0, True)
            second(S // 2 - 1, 1, True)

        def in_pairs(eng, body, last=S):
            body(0, 0, False)
            body(0, 1, False)
            with eng.Fori(1, last // 2) as half:
                for par in range(2):
                    body(half, par, True)
        n_consts = 16 * len(given)
        chunks = [(i, min(T, CAP - i)) for i in range(0, CAP, T)]

        PARTS = 3 + 3 * FH + 3

        def fourth(eng, first, expert, attention):
            def with_experts(half, par):
                first(half + 2, par)
                expert(half, 0)
                expert(half, 1)
                attention(half + 2, par)

            for s in (0, 1):
                first(s, s)
                attention(s, s)
            with_experts(0, 0)
            with eng.Fori(0, E // 4 - 1) as j:
                with_experts(2 * j + 1, 1)
                with_experts(2 * j + 2, 0)
            with_experts(E // 2 - 1, 1)
            for s in (S - 2, S - 1):
                first(s, s % 2)
                attention(s, s % 2)

        def few(s):
            return TT if isinstance(s, int) and s not in BUSY else FEW_TILES

        def counted(s, of_batch):
            if isinstance(s, int):
                return sum(of_batch(i) for i in range(s))
            each = of_batch(LOOP.start)
            return each * s + (counted(LOOP.start, of_batch) - each * LOOP.start)

        helped_qk = lambda i: HELPED_QK[i]
        own_qk = lambda i: TT - HELPED_QK[i]
        vector_sums = lambda i: TT - 1 - (QK_TILES if i in SUMMED_QK else 0)

        def help_before(s, helped):
            return min(max(s - helped.start, 0), len(helped)) if isinstance(s, int) else s - helped.start

        def value_products(eng, half, par, lg):
            at = (2 * par + lg) * GW + (QH + 1) * HD
            for t in range(S):
                i = eng.tensor_tensor(from_key(1, par, t)[:, lg].rearrange("p (s q d) -> p s q d", q=QH, d=HD), sc2[:, lg, t, t:S, :].unsqueeze(3).broadcast_to([P, S - t, QH, HD]),
                                      qkv_t[:, t, half, at:at + HD].unsqueeze(1).unsqueeze(1).broadcast_to([P, S - t, QH, HD]), ALU.mult)
            return i

        def qk_product(eng, dst, s, sp, a):
            at = slice(a * D, (a + 1) * D)
            return eng.tensor_tensor(dst.rearrange("p (h g d) -> p h g d", h=H, g=H),
                                     q_all[:, s, at].rearrange("p (h d) -> p h d", d=HD).unsqueeze(2).broadcast_to([P, H, H, HD]),
                                     k_all[:, s, at].rearrange("p (g d) -> p g d", d=HD).unsqueeze(1).broadcast_to([P, H, H, HD]), ALU.mult)

        def qk_product_wide(eng, dst, s, sp, a):
            at = slice(a * D, (a + 1) * D)
            return eng.tensor_tensor(dst.rearrange("p (d h g) -> p d h g", h=H, g=H),
                                     q_all[:, s, at].rearrange("p (h d) -> p d h", d=HD).unsqueeze(3).broadcast_to([P, HD, H, H]),
                                     k_all[:, s, at].rearrange("p (g d) -> p d g", d=HD).unsqueeze(2).broadcast_to([P, HD, H, H]), ALU.mult)

        def pv_product(eng, s, sp, a):
            return eng.tensor_tensor(value_buf[a].rearrange("p (g h d) -> p g h d", g=H, h=H),
                                     score[:, sp, a * H * H:(a + 1) * H * H].rearrange("p (h g) -> p g h", g=H).unsqueeze(3)
                                     .broadcast_to([P, H, H, HD]),
                                     v_all[:, s, a * D:(a + 1) * D].rearrange("p (d g) -> p g d", g=H).unsqueeze(2)
                                     .broadcast_to([P, H, H, HD]), ALU.mult)

        @block.sync
        def _(sp):
            for s in range(S):
                sp.dma_start(xn_all[:, s], x[s].rearrange("(a p) d -> p a d", p=P)).then_inc(x_in[s // CHUNK], 16)
            for n, src in given.items():
                sp.dma_start(C[n][:], src).then_inc(W["consts_in"], 16)
            sp.wait_ge(W["zero_done"], 1)
            for k in range(CT):
                sp.dma_start(slots_d[k * E * P:(k + 1) * E * P, :].rearrange("(p a) d -> p a d", p=P),
                             zeros[:].broadcast_to([P, E, D])).then_inc(W["zero_out"], 16)

            def load(half, par):
                e = ev(half, par)
                sp.dma_start(w1_sb[:, par], w1[e]).then_inc(w_in[par], 16)
                sp.dma_start(w2_sb[:, par], w2[e].rearrange("(f p) d -> p f d", p=P)).then_inc(w_in[par], 16)
                sp.dma_start(xe[:, par], slots_d[bass.ds(e * CAP, CAP), :].rearrange("(a p) d -> p a d", p=P)).then_inc(xe_in[par], 16)

            def store(half, par):
                e = ev(half, par)
                sp.wait_ge(W["part_kept"], PARTS * (e + 1))
                sp.dma_start(expert_d[bass.ds(e * CAP, CAP), :].rearrange("(a p) d -> p a d", p=P), ye[:, par]).then_inc(ye_out[par], 16)

            sp.wait_ge(W["index_done"], 1)
            sp.wait_ge(W["z2_kept"], S)
            sp.wait_ge(W["scattered"], 16 * NT * TOPK)
            load(0, 0)
            load(0, 1)
            with sp.Fori(0, E // 2 - 1) as half:
                for par in range(2):
                    store(half, par)
                    load(half + 1, par)
            store(E // 2 - 1, 0)
            store(E // 2 - 1, 1)

            sp.wait_ge(W["score_done"], S)
            sp.wait_ge(W["score_sum"], QK_TILES * len(SUMMED_QK))
            sp.dma_start(xr, x.rearrange("s (a p) d -> p (s a) d", p=P).rearrange("p (s a) d -> p s a d", a=TT)).then_inc(W["tail_in"], 16)
            with sp.Fori(0, S // 2) as half:
                for par in range(2):
                    s = ev(half, par)
                    sp.wait_ge(W["res_done"], s + 1)
                    sp.dma_start(out[s].rearrange("(a p) d -> p a d", p=P), xr[:, s]).then_inc(y_out[par], 16)
            for par in range(2):
                sp.wait_ge(y_out[par], 16 * (S // 2))

        @block.vector
        def _(dve):
            V = nc.vector
            V.memset(zeros[:], 0.0).then_inc(W["zero_done"], 1)
            V.memset(eps[:], EPS)
            V.memset(latT[LAT:LAT + 1], 1.0)
            V.memset(sc, NEG).then_inc(W["filled"], 1)

            count = {"moments": 0, "route": 0}

            def link(name, ins):
                ins.then_inc(W[name], 1)
                count[name] += 1
                dve.wait_ge(W[name], count[name])

            def statistics(first, last):
                with dve.Fori(first, last) as s:
                    for a in range(TT):
                        i = V.bn_stats(stat[:, s * TT + a, :], xn_all[:, s, a, :])
                    i.then_inc(W["moments"], 1)
                count["moments"] += last - first
                dve.wait_ge(W["moments"], count["moments"])

            def deviations(first, last, row, devs):
                J = slice(first * TT, last * TT)
                even, odd = stat[:, J, 1], stat[:, J, 4]
                mean, inv, dif, sq = (mom[:, r, J] for r in (row, row + 1, 4, 5))
                V.tensor_tensor(mean, even, odd, ALU.add)
                V.tensor_tensor(dif, even, odd, ALU.subtract)
                link("moments", V.tensor_tensor(sq, stat[:, J, 2], stat[:, J, 5], ALU.add))
                V.tensor_scalar(mean, mean, 0.5, None, ALU.mult)
                link("moments", V.tensor_tensor(dif, dif, dif, ALU.mult))
                V.scalar_tensor_tensor(inv, dif, float(D // 4), sq, ALU.mult, ALU.add).then_inc(W["moments"], 1)
                count["moments"] += 1
                dve.wait_ge(W["dev_done"], devs)
                link("moments", V.reciprocal(inv, inv))

            for c in range(2):
                first, last = c * CHUNK, (c + 1) * CHUNK
                dve.wait_ge(x_in[c], 16 * CHUNK)
                statistics(first, last)
                deviations(first, last, 0, 2 * c + 1)
                with dve.Fori(first, last) as s:
                    for a in range(TT):
                        i = V.tensor_scalar(xn_all[:, s, a, :], xn_all[:, s, a, :], mom[:, 0, bass.ds(s * TT + a, 1)],
                                            mom[:, 1, bass.ds(s * TT + a, 1)], ALU.subtract, ALU.mult)
                    i.then_inc(W["norm1"], 1)
                dve.wait_ge(W["norm1"], last)
                statistics(first, last)
                deviations(first, last, 2, 2 * c + 2)
                for s in range(first, last):
                    if s >= CHUNK:
                        dve.wait_ge(W["zT_ready"], s - CHUNK + 1)
                    for a in range(TT):
                        i = V.tensor_scalar(zb[:, s % CHUNK, a, :], xn_all[:, s, a, :], mom[:, 2, s * TT + a:s * TT + a + 1],
                                            mom[:, 3, s * TT + a:s * TT + a + 1], ALU.subtract, ALU.mult)
                    i.then_inc(W["zb_done"], 1)

            halves = lambda v: v.rearrange("p (m two f) -> p m two f", two=2, f=HD // 2)

            def unit(half, par, steady):
                u = ev(half, par)
                some = steady or par
                dve.wait_ge(W["qk_prod"], u + 1)
                for t in range(S):
                    i = V.tensor_reduce(sc[:, :, t, t:S, :].rearrange("p l s q -> p l (s q)"), from_key(0, par, t).rearrange("p l (m d) -> p l m d", d=HD),
                                        AX_X, ALU.add)
                i.then_inc(W["qk_score"], 1)
                dve.wait_ge(W["qk_score"], u + 1)
                V.tensor_reduce(smax, sc.rearrange("p l t s q -> p l (s q) t"), AX_X, ALU.max).then_inc(W["s_max"], 1)
                dve.wait_ge(W["s_max"], u + 1)
                if some:
                    wait_past(dve, "pv_prod", u)
                V.tensor_tensor(sc2.rearrange("p l t s q -> p l t (s q)"), sc.rearrange("p l t s q -> p l t (s q)"),
                                smax.unsqueeze(2).broadcast_to([P, 2, S, S * QH]), ALU.subtract).then_inc(W["s_diff"], 1)
                dve.wait_ge(W["s_exp"], u + 1)
                V.tensor_reduce(ssum, sc2.rearrange("p l t s q -> p l (s q) t"), AX_X, ALU.add).then_inc(W["s_sum"], 1)
                dve.wait_ge(W["s_sum"], u + 1)
                V.reciprocal(ssum, ssum).then_inc(W["s_rsum"], 1)
                dve.wait_ge(W["s_rsum"], u + 1)
                V.tensor_tensor(sc2.rearrange("p l t s q -> p l t (s q)"), sc2.rearrange("p l t s q -> p l t (s q)"),
                                ssum.unsqueeze(2).broadcast_to([P, 2, S, S * QH]), ALU.mult).then_inc(W["s_prob"], 1)
                if steady:
                    dve.wait_ge(W["pv_ready"], u - 1)
                dve.wait_ge(W["s_prob"], u + 1)
                value_products(V, half, par, 0).then_inc(W["pv_own"], 1)
                if some:
                    rotate_q(u - 1, not steady)

            def rotate_q(s, first):
                q = q_all[:, s, :]
                dve.wait_ge(W["q_done"], s + 1)
                if not first:
                    dve.wait_ge(W["rope_q"], s)
                V.tensor_tensor(t1[:, 0], q, C["cos"][:], ALU.mult)
                V.tensor_tensor(halves(t2[:, 0])[:, :, 0, :], halves(q)[:, :, 1, :], halves(C["sin"][:])[:, :, 0, :], ALU.mult)
                V.tensor_tensor(halves(t2[:, 0])[:, :, 1, :], halves(q)[:, :, 0, :], halves(C["sin"][:])[:, :, 1, :],
                                ALU.mult).then_inc(W["q_read"], 1)
                dve.wait_ge(W["q_read"], s + 1)
                V.tensor_tensor(q, t1[:, 0], t2[:, 0], ALU.add).then_inc(W["rope_q"], 1)

            in_pairs(dve, unit)
            rotate_q(S - 1, False)
            def rotated(half, par):
                s = ev(half, par)
                dve.wait_ge(W["rope_k"], s + 1)
                V.tensor_tensor(k_all[:, s, :], turned_k[par][0], turned_k[par][1], ALU.add).then_inc(W["roped_k"], 1)

            def residual(half, par, steady):
                s = ev(half, par)
                dve.wait_ge(W["proj_ready"], s + 1)
                V.tensor_tensor(xn_all[:, s], bank[2 + par][:].rearrange("p (a d) -> p a d", a=TT), xn_all[:, s], ALU.add).then_inc(W["h1_done"], 1)
                dve.wait_ge(W["h1_done"], s + 1)
                for a in range(TT):
                    i = V.bn_stats(stat[:, s * TT + a, :], xn_all[:, s, a, :])
                i.then_inc(W["moments"], 1)
                rotated(half, par)

            in_pairs(dve, residual)
            count["moments"] += S
            dve.wait_ge(W["moments"], count["moments"])
            deviations(0, S, 0, 5)

            for s in range(S):
                if s >= CHUNK:
                    dve.wait_ge(W["z2_kept"], s - CHUNK + 1)
                    dve.wait_ge(W["z2T_ready"], s - CHUNK + 1)
                for a in range(TT):
                    n = s * TT + a
                    i = V.tensor_scalar(zb[:, s % CHUNK, a, :], xn_all[:, s, a, :], mom[:, 0, n:n + 1], mom[:, 1, n:n + 1], ALU.subtract, ALU.mult)
                i.then_inc(W["z2_done"], 1)
            def scores(s, sp):
                kind = s if isinstance(s, int) else LOOP.start
                summed = QK_TILES if kind in SUMMED_QK else 0
                own = TT - HELPED_QK[kind]
                order = [a for a in ((0, 2, 1, 3) if summed else (0, 1, 2, 3)) if a < own]
                buf = {0: 0, 1: 1, 2: 1, 3: 0}
                assert summed or own <= 2
                sums = counted(s, vector_sums)

                def product(a):
                    (qk_product_wide if a < summed else qk_product)(V, prodA[:, buf[a], :], s, sp, a).then_inc(W["prod_done"], 1)

                def total(a):
                    nonlocal sums
                    if a < own:
                        dve.wait_ge(W["prod_done"], counted(s, own_qk) + order.index(a) + 1)
                        src = prodA[:, buf[a], :]
                    else:
                        dve.wait_ge(W["help_qk"], counted(s, helped_qk) + a - own + 1)
                        src = help_buf[kind][a]
                    i = V.tensor_reduce(score[:, sp, a * H * H:(a + 1) * H * H], src.rearrange("p (m d) -> p m d", d=HD), AX_X, ALU.add)
                    i.then_inc(W["score_done" if a == TT - 1 else "sum_done"], 1)
                    sums = sums + 1

                if kind > 0:
                    dve.wait_ge(W["sum_done"], sums)
                    dve.wait_ge(W["score_done"], s)
                    if kind - 1 in SUMMED_QK:
                        dve.wait_ge(W["score_sum"], QK_TILES * len([i for i in SUMMED_QK if i < kind]))
                product(0)
                if summed and own > 2:
                    product(2)
                    total(2)
                    dve.wait_ge(W["sum_done"], sums)
                    product(1)
                    if own > 3:
                        dve.wait_ge(W["score_sum"], QK_TILES * SUMMED_QK.index(kind) + 1)
                        product(3)
                    total(3)
                else:
                    product(1)
                    for a in range(summed, TT):
                        total(a)

            dve.wait_ge(W["roped_k"], S)
            dve.wait_ge(W["rope_q"], S)
            dve.wait_ge(W["v_done"], S)
            scores(0, 0)

            dve.wait_ge(W["logit_ready"], S)
            V.tensor_copy(logit[:].rearrange("p n e -> p (n e)"), bank[6][:, 0:NT * E]).then_inc(W["logit_kept"], 1)

            def step(ins):
                link("route", ins)

            lg = logit[:]
            full = lambda v: v[:].unsqueeze(2).broadcast_to([P, NT, E])
            each = lambda v: v[:].unsqueeze(1).broadcast_to([P, NT, E])
            dve.wait_ge(W["logit_kept"], 1)
            for k in range(TOPK):
                step(V.tensor_reduce(best[:, k, :], lg, AX_X, ALU.max))
                step(V.tensor_tensor(tmp8, lg, best[:, k, :].unsqueeze(2).broadcast_to([P, NT, E]), ALU.is_equal))
                step(V.tensor_tensor(tmp8, tmp8, each(C["rev8"]), ALU.mult))
                step(V.tensor_reduce(tmp1[:], tmp8, AX_X, ALU.max))
                step(V.tensor_tensor(onehot[:, k], tmp8, full(tmp1), ALU.is_equal))
                if k == 0:
                    step(V.scalar_tensor_tensor(lg, onehot[:, 0], NEG, lg, ALU.mult, ALU.add))
            V.tensor_tensor(tmp1[:], best[:, 1, :], best[:, 0, :], ALU.subtract).then_inc(W["diff_done"], 1)
            dve.wait_ge(W["route_exp"], 1)
            step(V.tensor_scalar(tmp1[:], gate[:, 1, :], 1.0, None, ALU.add))
            step(V.reciprocal(gate[:, 0, :], tmp1[:]))
            step(V.tensor_tensor(gate[:, 1, :], gate[:, 1, :], gate[:, 0, :], ALU.mult))
            V.tensor_tensor(mask16[:], onehot[:, 0], onehot[:, 1], ALU.add).then_inc(W["mask_done"], 1)
            dve.wait_ge(W["pos_ready"], 1)
            tot = bank[1][:, 0:NT * E].rearrange("p (n e) -> p n e", e=E)
            pos = bank[0][:, 0:NT * E].rearrange("p (n e) -> p n e", e=E)
            step(V.tensor_copy(cum[:, 0], tot))
            src, sh = 0, 1
            while sh < NT:
                step(V.tensor_copy(cum[:, 1 - src, 0:sh, :], cum[:, src, 0:sh, :]))
                step(V.tensor_tensor(cum[:, 1 - src, sh:, :], cum[:, src, sh:, :], cum[:, src, 0:NT - sh, :], ALU.add))
                src, sh = 1 - src, 2 * sh
            step(V.tensor_tensor(cum[:, src], cum[:, src], tot, ALU.subtract))
            step(V.tensor_tensor(cum[:, src], cum[:, src], pos, ALU.add))
            place, fits = cum[:, src], cum[:, 1 - src]
            step(V.tensor_scalar(fits, place, float(CAP), None, ALU.is_lt))
            step(V.tensor_tensor(place, place, each(C["ebase"]), ALU.add))
            for k in range(TOPK):
                step(V.tensor_tensor(tmp8, onehot[:, k], fits, ALU.mult))
                step(V.tensor_reduce(fit1[:], tmp8, AX_X, ALU.add))
                step(V.tensor_tensor(gate[:, k, :], gate[:, k, :], fit1[:], ALU.mult))
                step(V.tensor_tensor(tmp8, tmp8, place, ALU.mult))
                step(V.tensor_reduce(tmp1[:], tmp8, AX_X, ALU.add))
                step(V.tensor_copy(gather_at[:, k, :], tmp1[:]))
                dmp = C["dump"][:].rearrange("p (k n) -> p k n", k=TOPK)[:, k, :]
                step(V.tensor_tensor(tmp1[:], tmp1[:], dmp, ALU.add))
                step(V.tensor_tensor(fit1[:], fit1[:], dmp, ALU.mult))
                step(V.tensor_tensor(tmp1[:], tmp1[:], fit1[:], ALU.subtract))
                step(V.tensor_copy(scatter_at[:, k, :], tmp1[:]))
            V.tensor_copy(fit1[:], tmp1[:]).then_inc(W["index_done"], 1)

            def combine(half, par, steady):
                s = ev(half, par)
                h1 = xn_all[:, s]
                if steady:
                    dve.wait_ge(W["f_step"], 2 * s - 2)
                V.tensor_copy(gate_s[:, par], gate[:].rearrange("p k (s a) -> p k s a", a=TT)[:, :, s, :]).then_inc(W["gate_in"], 1)
                dve.wait_ge(W["gate_in"], s + 1)
                dve.wait_ge(gathered[par], 16 * TT * TOPK * (half + 1))
                for k in range(TOPK):
                    for a in range(TT):
                        i = V.scalar_tensor_tensor(h1[:, a, :], yg[:, s, a, k, :], gate_s[:, par, k, a:a + 1], h1[:, a, :], ALU.mult, ALU.add)
                    i.then_inc(W["f_step"], 1)
                    dve.wait_ge(W["f_step"], TOPK * s + k + 1)

            def made(s, helped):
                return TT * s - help_before(s, helped)

            rows = lambda v: v.rearrange("p (m g) -> p m g", g=H)

            def normalize(s, par):
                dve.wait_ge(W["value_sum"], s + 1)
                if few(s) < TT:
                    dve.wait_ge(W["value_part"], s - BUSY.start + 1)
                if not isinstance(s, int) or s >= 2:
                    dve.wait_ge(W["ao_ready"], s - 1)
                tiles = few(s)
                for src, a, b in ((bank[7][:].rearrange("p (a d) -> p a d", d=D), 0, tiles), (ao[:, par], tiles, TT)):
                    if b > a:
                        i = V.tensor_tensor(ao[:, par, a:b].rearrange("p a (h d) -> p (a h) d", d=HD),
                                            src[:, a:b].rearrange("p a (h d) -> p (a h) d", d=HD),
                                            hsum[:, par, a * H:b * H].unsqueeze(2).broadcast_to([P, (b - a) * H, HD]), ALU.mult)
                i.then_inc(W["ao_done"], 1)

            def branch_out(s):
                dve.wait_ge(W["attn_ready"], s + 1)
                V.tensor_tensor(q_all[:, s, :].rearrange("p (a d) -> p a d", a=TT), bank[4][:].rearrange("p (a d) -> p a d", a=TT),
                                C["bout"][:].unsqueeze(1).broadcast_to([P, TT, D]), ALU.add).then_inc(W["attn_done"], 1)

            def batch(par, s, helped, made_pv):
                later = lambda n: not isinstance(s, int) or s >= n
                dve.wait_ge(W["score_done"], s + 1)
                n = QK_TILES if isinstance(s, int) and s in SUMMED_QK else 0
                if n:
                    dve.wait_ge(W["score_sum"], QK_TILES * (SUMMED_QK.index(s) + 1))
                parts = [(rows(bank[5][:, 0:n * H * H]), 0, n)] * (n > 0) + [(rows(score[:, par, n * H * H:]), n, TT)]
                for src, a, b in parts:
                    i = V.tensor_reduce(hmax[:, par, a * H:b * H], src, AX_X, ALU.max)
                i.then_inc(W["row_max"], 1)
                dve.wait_ge(W["row_max"], s + 1)
                for src, a, b in parts:
                    i = V.tensor_tensor(rows(score[:, par, a * H * H:b * H * H]), src,
                                        hmax[:, par, a * H:b * H].unsqueeze(2).broadcast_to([P, (b - a) * H, H]), ALU.subtract)
                i.then_inc(W["row_diff"], 1)
                if not isinstance(s, int) or s + 1 < S:
                    if later(1):
                        dve.wait_ge(W["value_prod"], made_pv)
                    if later(HELPED_PV.start + 1):
                        dve.wait_ge(W["help_pv"], help_before(s, HELPED_PV))
                    scores(s + 1, 1 - par)
                if later(2):
                    branch_out(s - 2)
                if later(1):
                    normalize(s - 1, 1 - par)
                dve.wait_ge(W["row_exp"], s + 1)
                if later(2):
                    dve.wait_ge(W["ao_done"], s - 1)
                V.tensor_reduce(hsum[:, par, :], rows(score[:, par]), AX_X, ALU.add).then_inc(W["row_sum"], 1)
                dve.wait_ge(W["row_sum"], s + 1)
                V.reciprocal(hsum[:, par, :], hsum[:, par, :]).then_inc(W["row_inv"], 1)
                if later(1):
                    dve.wait_ge(W["value_sum"], s)
                else:
                    dve.wait_ge(W["score_done"], 2)
                if later(BUSY.start + 1):
                    dve.wait_ge(W["value_part"], (s if not isinstance(s, int) else min(s, BUSY.stop)) - BUSY.start)
                if few(s) < TT:
                    dve.wait_ge(W["ao_ready"], s - 1)
                own = TT - 1 if helped else TT
                for a in range(own):
                    pv_product(V, s, par, a).then_inc(W["value_prod"], 1)
                for a in range(few(s), TT):
                    if a < own:
                        dve.wait_ge(W["value_prod"], made(s, HELPED_PV) + a + 1)
                    else:
                        dve.wait_ge(W["help_pv"], help_before(s, HELPED_PV) + 1)
                    i = V.tensor_reduce(ao[:, par, a, :], value_buf[a].rearrange("p (g m) -> p m g", g=H), AX_X, ALU.add)
                if few(s) < TT:
                    i.then_inc(W["value_part"], 1)
                dve.wait_ge(W["row_inv"], s + 1)

            def fixed(s):
                batch(s % 2, s, s in HELPED_PV, made(s, HELPED_PV))
            fixed(0)
            fixed(1)
            fixed(2)
            with dve.Fori(1, S // 2 - 2) as half:
                for par in (1, 0):
                    s = 2 * half + 2 - par
                    batch(par, s, True, made(s, HELPED_PV))
            fixed(S - 3)
            fixed(S - 2)
            in_pairs(dve, combine, S // 2)
            fixed(S - 1)

            def gated(half, par):
                s = ev(half, par)
                dve.wait_ge(W["silu_done"], s + 1)
                dve.wait_ge(W["attn_done"], s + 1)
                V.tensor_tensor(gb[:, par].rearrange("p a d -> p (a d)"), gb[:, par].rearrange("p a d -> p (a d)"), q_all[:, s, :], ALU.mult).then_inc(W["gate_done"], 1)
                dve.wait_ge(W["gate_done"], s + 1)
                dve.wait_ge(W["tail_in"], 16)
                V.tensor_tensor(xr[:, s], xr[:, s], gb[:, par], ALU.add).then_inc(W["res_done"], 1)

            branch_out(S - 2)
            normalize(S - 1, 1)
            with dve.Fori(S // 4, S // 2 - 1) as half:
                for par in range(2):
                    combine(half, par, True)
                    gated(2 * half - S // 2 + par, 0)
                    gated(2 * half - S // 2 + par, 1)
            branch_out(S - 1)
            for par in range(2):
                combine(S // 2 - 1, par, True)
                gated(S // 2 - 2 + par, 0)
                gated(S // 2 - 2 + par, 1)

        @block.tensor
        def _(pe):
            M = nc.tensor
            pe.wait_ge(W["consts_in"], n_consts)
            pe.wait_ge(W["filled"], 1)

            def transposes(dst, src):
                for a in range(TT):
                    i = M.transpose(dst[:, a * P:(a + 1) * P], src[:, a, :], C["identf"][:])
                return i

            def projected(dst, src, weight, width=D, stop=True):
                for a in range(TT):
                    i = M.matmul(dst[:, a * width:(a + 1) * width], src[:, a * P:(a + 1) * P], weight[:], start=True, stop=stop)
                return i

            def turn(s):
                pe.wait_ge(W["zb_done"], s + 1)
                if s >= 2:
                    pe.wait_ge(W["lnT_done"], s - 1)
                transposes(bank[s % 2], zb[:, s % CHUNK]).then_inc(W["zT_ready"], 1)

            def block_qkv(s):
                pe.wait_ge(W["lnT_done"], s + 1)
                if s >= 2:
                    pe.wait_ge(W["bqkv_done"], s - 1)
                for a in range(TT):
                    i = M.matmul(bank[2 + 2 * (s % 2) + a // 2][:, (a % 2) * QKV:(a % 2 + 1) * QKV], lnT[:, s % 2, a * P:(a + 1) * P],
                                 C["wqkv"][:], start=True, stop=True)
                i.then_inc(W["bqkv_ready"], 1)

            turn(0)
            for s in range(S):
                if s + 1 < S:
                    turn(s + 1)
                block_qkv(s)

            def turn_branch(half, par, steady):
                s = ev(half, par)
                pe.wait_ge(W["xnb_done"], s + 1)
                if steady or par:
                    pe.wait_ge(W["xnT_done"], s)
                transposes(bank[0], xnb[:, par]).then_inc(W["xnT_ready"], 1)

            def project_branch(half, par, steady):
                s = ev(half, par)
                later = steady or par
                pe.wait_ge(W["xnT_done"], s + 1)
                if later:
                    pe.wait_ge(W["lat_done"], s)
                M.matmul(bank[4][0:LAT, :], C["wdown"][:], xnT[:, par, :], start=True, stop=True).then_inc(W["lat_ready"], 1)
                if later:
                    pe.wait_ge(W["q_done"], s)
                for a in range(TT):
                    dst = bank[5][:, a * D:(a + 1) * D]
                    M.matmul(dst, xnT[:, par, a * P:(a + 1) * P], C["wq"][:], start=True, stop=False)
                    i = M.matmul(dst, C["ones1"][:], C["bq"][:], start=False, stop=True)
                i.then_inc(W["q_ready"], 1)
                pe.wait_ge(W["lat_done"], s + 1)
                if later:
                    pe.wait_ge(W["k_done"], s)
                projected(bank[6], latT[0:LAT + 1, par, :], C["wupk"]).then_inc(W["k_ready"], 1)
                if later:
                    pe.wait_ge(W["v_done"], s)
                projected(bank[7], latT[0:LAT + 1, par, :], C["wupv"]).then_inc(W["v_ready"], 1)

            def value_sums(half, par):
                u = ev(half, par)
                pe.wait_ge(W["pv_own"], u + 1)
                pe.wait_ge(W["pv_prod"], u + 1)
                wait_past(pe, "block_kept", u)
                total = bank[1][:].rearrange("p (l s w) -> p l s w", l=2, s=S)
                for t in range(S):
                    i = M.matmul(total[:, :, t:S, :], C["identf"][:], from_key(1, par, t).rearrange("p l (s w) -> p l s w", w=QH * HD),
                                 start=(t == 0), stop=(t == S - 1))
                i.then_inc(W["pv_ready"], 1)

            def second_stage(half, par, steady):
                turn_branch(half, par, steady)
                if steady or par:
                    value_sums(half if par else half - 1, 1 - par)
                project_branch(half, par, steady)

            pe.wait_ge(W["bqkv_done"], S)
            in_pairs(pe, second_stage)
            value_sums(S // 2 - 1, 1)

            def turn_block(half, par, steady):
                s = ev(half, par)
                pe.wait_ge(W["aoc_done"], s + 1)
                if steady:
                    pe.wait_ge(W["bT_done"], s - 1)
                transposes(bank[par], aoc[:, par]).then_inc(W["bT_ready"], 1)

            def project_block(half, par, steady):
                s = ev(half, par)
                pe.wait_ge(W["bT_done"], s + 1)
                if steady:
                    pe.wait_ge(W["h1_done"], s - 1)
                projected(bank[2 + par], bT, C["wproj"]).then_inc(W["proj_ready"], 1)

            pe.wait_ge(W["xnT_done"], S)
            pe.wait_ge(W["block_kept"], S)
            staggered(pe, turn_block, project_block)
            pe.wait_ge(W["q_done"], S)
            pe.wait_ge(W["v_done"], S)
            pe.wait_ge(W["k_done"], S)

            def turn_normed(s):
                pe.wait_ge(W["z2_done"], s + 1)
                if s >= 2:
                    pe.wait_ge(W["x2T_done"], s - 1)
                transposes(bank[4 + s % 2], zb[:, s % CHUNK]).then_inc(W["z2T_ready"], 1)

            turn_normed(0)
            for s in range(S):
                if s + 1 < S:
                    turn_normed(s + 1)
                pe.wait_ge(W["x2T_done"], s + 1)
                projected(bank[6][:, s * TT * E:(s + 1) * TT * E], lnT[:, s % 2, :], C["wrouter"], E).then_inc(W["logit_ready"], 1)

            def sum_scores(s):
                if s > 0:
                    pe.wait_ge(W["row_diff"], s)
                for a in range(QK_TILES):
                    pe.wait_ge(W["prod_done"], counted(s, own_qk) + 1 + (0 if a == 0 else 1 if own_qk(s) == 2 else 2))
                    for d in range(HD):
                        i = M.matmul(bank[5][:, a * H * H:(a + 1) * H * H], C["identf"][:], prodA[:, a, d * H * H:(d + 1) * H * H],
                                     start=(d == 0), stop=(d == HD - 1))
                    i.then_inc(W["score_sum"], 1)

            pe.wait_ge(W["x2T_done"], S)
            sum_scores(0)
            pe.wait_ge(W["mask_done"], 1)
            mask = mask16[:].rearrange("p n e -> p (n e)")
            M.matmul(bank[0][:, 0:NT * E], C["tri"][:], mask, start=True, stop=True)
            M.matmul(bank[1][:, 0:NT * E], C["allones"][:], mask, start=True, stop=True).then_inc(W["pos_ready"], 1)
            pe.wait_ge(W["index_done"], 1)

            def expert(half, par):
                e = ev(half, par)

                def free(k):
                    if not isinstance(e, int) or PARTS * e + k >= BANKS:
                        pe.wait_ge(W["part_kept"], PARTS * e + k - BANKS + 1)
                    return bank[k % BANKS]

                pe.wait_ge(xe_in[par], 16 * (half + 1))
                pe.wait_ge(w_in[par], 32 * (half + 1))
                for q in range(3):
                    dst = free(q)
                    for a in range(4 * q, min(4 * q + 4, CT)):
                        i = M.transpose(dst[:, (a % 4) * P:(a % 4 + 1) * P], xe[:, par, a, :], C["identf"][:])
                    i.then_inc(W["part_ready"], 1)
                for f in range(FH):
                    for m, (at, n) in enumerate(chunks):
                        dst = free(3 + 3 * f + m)
                        pe.wait_ge(W["part_kept"], PARTS * e + m + 1)
                        M.matmul(dst[:, 0:n], w1_sb[:, par, f * P:(f + 1) * P], xeT[:, at:at + n],
                                 start=True, stop=True).then_inc(W["part_ready"], 1)
                for q in range(3):
                    dst = free(3 + 3 * FH + q)
                    pe.wait_ge(W["part_kept"], PARTS * e + 3 + 3 * (FH - 1) + q + 1)
                    for a in range(4 * q, min(4 * q + 4, CT)):
                        for f in range(FH):
                            i = M.matmul(dst[:, (a % 4) * P:(a % 4 + 1) * P], hT[:, f, a * P:(a + 1) * P],
                                         w2_sb[:, par, f, :], start=(f == 0), stop=(f == FH - 1))
                    i.then_inc(W["part_ready"], 1)

            def turn_out(s, par):
                pe.wait_ge(W["ao_done"], s + 1)
                wait_past(pe, "attn_done", s)
                transposes(bank[4], ao[:, par]).then_inc(W["ao_ready"], 1)

            def project_out(s):
                pe.wait_ge(W["aoT_done"], s + 1)
                projected(bank[4], aoT, C["wout"]).then_inc(W["attn_ready"], 1)

            def sum_values(s, tiles):
                wait_past(pe, "ao_done", s)
                for a in tiles:
                    alone = isinstance(s, int) and s not in HELPED_PV
                    if a == TT - 1 and not alone:
                        pe.wait_ge(W["help_pv"], help_before(s, HELPED_PV) + 1)
                    else:
                        pe.wait_ge(W["value_prod"], TT * s - help_before(s, HELPED_PV) + a + 1)
                    for g in range(H):
                        i = M.matmul(bank[7][:, a * D:(a + 1) * D], C["identf"][:], value_buf[a][:, g * D:(g + 1) * D],
                                     start=(g == 0), stop=(g == H - 1))
                return i

            def attention(s, par):
                later = not isinstance(s, int) or s >= 1
                if isinstance(s, int) and s + 1 in SUMMED_QK:
                    sum_scores(s + 1)
                if later:
                    turn_out(s - 1, 1 - par)
                tiles = range(few(s))
                last = sum_values(s, tiles[:2])
                if later:
                    project_out(s - 1)
                if few(s) > 2:
                    last = sum_values(s, tiles[2:])
                last.then_inc(W["value_sum"], 1)

            fourth(pe, lambda s, par: None, expert, attention)
            turn_out(S - 1, 1)
            project_out(S - 1)

        @block.scalar
        def _(act):
            A = nc.scalar

            def deviation(first, last, row, links):
                act.wait_ge(W["moments"], links)
                v = mom[:, row + 1, first * TT:last * TT]
                A.activation(v, v, ACT.Sqrt, bias=eps[:], scale=1.0 / D).then_inc(W["dev_done"], 1)

            act.wait_ge(W["filled"], 1)
            def root(c, row):
                deviation(c * CHUNK, (c + 1) * CHUNK, row, (2 * c + row // 2) * (CHUNK + 4) + CHUNK + 3)

            def keep_block_qkv(s):
                if s >= 2:
                    act.wait_ge(W["bqkv_ready"], s - 1)
                act.wait_ge(W["zT_ready"], s + 1)
                A.activation(lnT[:, s % 2, :], bank[s % 2][:], ACT.Identity, bias=C["ln1b"][:], scale=C["ln1w"][:]).then_inc(W["lnT_done"], 1)
                if s:
                    keep_qkv(s - 1)

            def keep_qkv(s):
                act.wait_ge(W["bqkv_ready"], s + 1)
                for k in range(2):
                    i = A.copy(qkv_t[:, s, 2 * k:2 * k + 2, :], bank[2 + 2 * (s % 2) + k][:, 0:2 * QKV].rearrange("p (a c) -> p a c", a=2))
                i.then_inc(W["bqkv_done"], 1)

            root(0, 0)
            root(0, 2)
            root(1, 0)
            act.wait_ge(W["consts_in"], n_consts)
            for s in range(CHUNK):
                keep_block_qkv(s)
            root(1, 2)
            for s in range(CHUNK, S):
                keep_block_qkv(s)
            keep_qkv(S - 1)
            n = 4 * (CHUNK + 4)

            def second_stage(half, par, steady):
                s = ev(half, par)
                if steady:
                    act.wait_ge(W["xnT_ready"], s - 1)
                A.copy(xnb[:, par], xn_all[:, s]).then_inc(W["xnb_done"], 1)
                act.wait_ge(W["s_diff"], s + 1)
                A.activation(sc2, sc2, ACT.Exp, scale=SCALE).then_inc(W["s_exp"], 1)
                if steady:
                    act.wait_ge(W["q_ready"], s - 1)
                act.wait_ge(W["xnT_ready"], s + 1)
                A.copy(xnT[:, par, :], bank[0][:]).then_inc(W["xnT_done"], 1)
                if steady:
                    act.wait_ge(W["v_ready"], s - 1)
                if steady or par:
                    keep_sums(half if par else half - 1, 1 - par)
                act.wait_ge(W["lat_ready"], s + 1)
                A.activation(latT[0:LAT, par, :], bank[4][0:LAT, :], ACT.Identity, bias=C["bdown"][:]).then_inc(W["lat_done"], 1)
                act.wait_ge(W["q_ready"], s + 1)
                A.copy(q_all[:, s, :], bank[5][:]).then_inc(W["q_done"], 1)
                act.wait_ge(W["k_ready"], s + 1)
                A.copy(k_all[:, s, :], bank[6][:]).then_inc(W["k_done"], 1)
                act.wait_ge(W["v_ready"], s + 1)
                A.copy(v_all[:, s, :], bank[7][:]).then_inc(W["v_done"], 1)

            def keep_sums(half, par):
                u = ev(half, par)
                at = 2 * par * GW
                act.wait_ge(W["pv_ready"], u + 1)
                A.copy(qkv_t[:, :, half, at:at + 2 * GW].rearrange("p s (l w) -> p l s w", l=2)[:, :, :, 0:QH * HD],
                       bank[1][:].rearrange("p (l s w) -> p l s w", l=2, s=S)).then_inc(W["block_kept"], 1)

            act.wait_ge(W["zb_done"], S)
            act.wait_ge(W["zT_ready"], S)
            in_pairs(act, second_stage)
            keep_sums(S // 2 - 1, 1)

            def copy_block(half, par, steady):
                s = ev(half, par)
                if steady:
                    act.wait_ge(W["bT_ready"], s - 1)
                A.copy(aoc[:, par].rearrange("p a (g w) -> p a g w", g=G),
                       qkv_t[:, s].rearrange("p a (g w) -> p a g w", g=G)[:, :, :, 0:QH * HD]).then_inc(W["aoc_done"], 1)

            def keep_block(half, par, steady):
                s = ev(half, par)
                act.wait_ge(W["bT_ready"], s + 1)
                wait_past(act, "proj_ready", s)
                A.copy(bT, bank[par][:]).then_inc(W["bT_done"], 1)

            act.wait_ge(W["block_kept"], S)
            staggered(act, copy_block, keep_block)
            deviation(0, S, 0, n + S + 3)

            act.wait_ge(W["aoc_done"], S)
            for s in range(S):
                act.wait_ge(W["z2T_ready"], s + 1)
                if s >= 2:
                    act.wait_ge(W["logit_ready"], s - 1)
                A.activation(lnT[:, s % 2, :], bank[4 + s % 2][:], ACT.Identity, bias=C["ln2b"][:], scale=C["ln2w"][:]).then_inc(W["x2T_done"], 1)
                act.wait_ge(W["z2_done"], s + 1)
                A.copy(z2_all[:, s], zb[:, s % CHUNK]).then_inc(W["z2_kept"], 1)

            act.wait_ge(W["diff_done"], 1)
            A.activation(gate[:, 1, :], tmp1[:], ACT.Exp).then_inc(W["route_exp"], 1)
            act.wait_ge(W["index_done"], 1)

            def expert(half, par):
                e = ev(half, par)
                wait_past(act, "part_ready", PARTS * e)
                for m, (at, n) in enumerate(chunks):
                    act.wait_ge(W["part_ready"], PARTS * e + m + 1)
                    A.activation(xeT[:, at:at + n], bank[m % BANKS][:, 0:n], ACT.Identity, bias=C["ln2b"][:], scale=C["ln2w"][:]).then_inc(W["part_kept"], 1)
                for f in range(FH):
                    for m, (at, n) in enumerate(chunks):
                        k = 3 + 3 * f + m
                        act.wait_ge(W["part_ready"], PARTS * e + k + 1)
                        A.activation(hT[:, f, at:at + n], bank[k % BANKS][:, 0:n], ACT.Gelu_apprx_tanh).then_inc(W["part_kept"], 1)
                wait_past(act, ye_out[par], 16 * half)
                for q in range(3):
                    k = 3 + 3 * FH + q
                    n = min(4, CT - 4 * q)
                    act.wait_ge(W["part_ready"], PARTS * e + k + 1)
                    A.copy(ye[:, par, 4 * q:4 * q + n, :], bank[k % BANKS][:, 0:n * D].rearrange("p (a d) -> p a d", d=D)).then_inc(W["part_kept"], 1)

            def keep_attention(s):
                act.wait_ge(W["ao_ready"], s + 1)
                wait_past(act, "attn_ready", s)
                A.copy(aoT[:], bank[4][:]).then_inc(W["aoT_done"], 1)

            def exponentials(s, par):
                act.wait_ge(W["row_diff"], s + 1)
                A.activation(score[:, par, :], score[:, par, :], ACT.Exp, scale=SCALE).then_inc(W["row_exp"], 1)

            def attention(s, par):
                if not isinstance(s, int) or s >= 1:
                    keep_attention(s - 1)

            fourth(act, exponentials, expert, attention)
            keep_attention(S - 1)

            def silu(half, par, steady):
                s = ev(half, par)
                act.wait_ge(W["f_step"], TOPK * (s + 1))
                if steady:
                    act.wait_ge(W["res_done"], s - 1)
                A.activation(gb[:, par], xn_all[:, s], ACT.Silu).then_inc(W["silu_done"], 1)

            in_pairs(act, silu)

        @block.gpsimd
        def _(pool):
            Q = nc.gpsimd
            halves = lambda v: v.rearrange("p (m two f) -> p m two f", two=2, f=HD // 2)
            pool.wait_ge(W["consts_in"], n_consts)
            def key_products(half, par, steady):
                u = ev(half, par)
                if steady:
                    pool.wait_ge(W["qk_score"], u - 1)
                for lg in range(2):
                    at = (2 * par + lg) * GW
                    for t in range(S):
                        i = Q.tensor_tensor(from_key(0, par, t)[:, lg].rearrange("p (s q d) -> p s q d", q=QH, d=HD),
                                            qkv_t[:, t:S, half, at:at + QH * HD].rearrange("p s (q d) -> p s q d", d=HD),
                                            qkv_t[:, t, half, at + QH * HD:at + (QH + 1) * HD].unsqueeze(1).unsqueeze(1)
                                            .broadcast_to([P, S - t, QH, HD]), ALU.mult)
                i.then_inc(W["qk_prod"], 1)

            def own_values(half, par, steady):
                u = ev(half, par)
                if steady:
                    pool.wait_ge(W["pv_ready"], u - 1)
                pool.wait_ge(W["s_prob"], u + 1)
                value_products(Q, half, par, 1).then_inc(W["pv_prod"], 1)

            pool.wait_ge(W["bqkv_done"], S)
            pool.wait_ge(W["filled"], 1)
            staggered(pool, key_products, own_values)

            def rotate(half, par, steady):
                s = ev(half, par)
                k, (with_cos, with_sin) = k_all[:, s, :], turned_k[par]
                if steady:
                    pool.wait_ge(W["roped_k"], s - 1)
                pool.wait_ge(W["k_done"], s + 1)
                Q.tensor_tensor(with_cos, k, C["cos"][:], ALU.mult)
                Q.tensor_tensor(halves(with_sin)[:, :, 0, :], halves(k)[:, :, 1, :], halves(C["sin"][:])[:, :, 0, :], ALU.mult)
                Q.tensor_tensor(halves(with_sin)[:, :, 1, :], halves(k)[:, :, 0, :], halves(C["sin"][:])[:, :, 1, :],
                                ALU.mult).then_inc(W["rope_k"], 1)

            in_pairs(pool, rotate)

            def help_scores(s, par):
                kind = s if isinstance(s, int) else LOOP.start
                if kind > 1:
                    pool.wait_ge(W["score_done"], s)
                for a in range(TT - HELPED_QK[kind], TT):
                    qk_product(Q, help_buf[kind][a], s, par, a).then_inc(W["help_qk"], 1)

            def help_values(s, par):
                pool.wait_ge(W["value_sum"], s)
                if not isinstance(s, int) or s > BUSY.start:
                    pool.wait_ge(W["value_part"], s - BUSY.start)
                pool.wait_ge(W["row_exp"], s + 1)
                pv_product(Q, s, par, TT - 1).then_inc(W["help_pv"], 1)

            pool.wait_ge(W["pv_ready"], S)
            pool.wait_ge(W["qk_score"], S)
            for s in range(2):
                pool.wait_ge(W["roped_k"], s + 1)
                pool.wait_ge(W["rope_q"], s + 1)
                help_scores(s, s)
            pool.wait_ge(W["roped_k"], S)
            pool.wait_ge(W["rope_q"], S)
            pool.wait_ge(W["v_done"], S)

            pool.wait_ge(W["zero_out"], 16 * CT)
            pool.wait_ge(W["index_done"], 1)
            pool.wait_ge(W["z2_kept"], S)
            for k in range(TOPK):
                for n in range(NT):
                    Q.indirect_dma_start(slots_d, bass.IndirectOffsetOnAxis(ap=scatter_at[:, k, n:n + 1], axis=0),
                                         z2_all[:, n // TT, n % TT, :], None).then_inc(W["scattered"], 16)
            pool.wait_ge(W["scattered"], 16 * NT * TOPK)
            help_scores(3, 1)
            help_values(2, 0)
            with pool.Fori(1, S // 2 - 2) as half:
                for par in (1, 0):
                    s = 2 * half + 2 - par
                    help_scores(s + 1, 1 - par)
                    help_values(s, par)
            help_scores(S - 2, 0)
            help_values(S - 3, 1)

            for par in range(2):
                pool.wait_ge(ye_out[par], 16 * (E // 2))
            for s in range(S):
                if s >= 2:
                    pool.wait_ge(gathered[s % 2], 16 * TT * TOPK * (s // 2))
                for a in range(TT):
                    for k in range(TOPK):
                        n = s * TT + a
                        Q.indirect_dma_start(yg[:, s, a, k, :], None, expert_d,
                                             bass.IndirectOffsetOnAxis(ap=gather_at[:, k, n:n + 1], axis=0)).then_inc(gathered[s % 2], 16)


def kernel(L0_attn_x, L0_attn_Wq, L0_attn_bq, L0_attn_Wdown, L0_attn_bdown, L0_attn_Wup, L0_attn_bup, L0_attn_Wout,
           L0_attn_bout, L0_ffn_ln1_weight, L0_ffn_ln1_bias, L0_ffn_ln2_weight, L0_ffn_ln2_bias, L0_ffn_qkv_weight,
           L0_ffn_proj_weight, L0_ffn_router_weight, L0_ffn_moe_w1, L0_ffn_moe_w2):
    import concourse.bacc as bacc
    import ml_dtypes
    from concourse.bass_utils import run_bass_kernel_spmd

    wup = np.concatenate([np.asarray(L0_attn_Wup), np.asarray(L0_attn_bup)[None]]).reshape(LAT + 1, H, 2, HD)
    col = lambda v: np.asarray(v).reshape(-1, 1)
    own = np.ascontiguousarray

    freq = (1.0 / 10000.0 ** (np.arange(0, HD, 2, dtype=np.float32) / np.float32(HD))).astype(np.float32)
    angle = (np.arange(T, dtype=np.float32)[:, None] * freq).reshape(TT, P, 1, 1, HD // 2).transpose(1, 0, 2, 3, 4)
    table = lambda first, second: own(np.broadcast_to(np.concatenate([first, second], 3), (P, TT, H, 2, HD // 2)), np.float32).reshape(P, TT * D)
    bf16 = ml_dtypes.bfloat16
    token = np.arange(NT)[None, None, :] * P + np.arange(P)[:, None, None]
    arrays = dict(
        x=np.asarray(L0_attn_x), wq=np.asarray(L0_attn_Wq), bq=np.asarray(L0_attn_bq)[None], wdown=np.asarray(L0_attn_Wdown),
        bdown=col(L0_attn_bdown), wupk=own(wup[:, :, 0].reshape(LAT + 1, D)), wupv=own(wup[:, :, 1].transpose(0, 2, 1)).reshape(LAT + 1, D),
        wout=np.asarray(L0_attn_Wout), bout=np.asarray(L0_attn_bout),
        ln1w=col(L0_ffn_ln1_weight), ln1b=col(L0_ffn_ln1_bias), ln2w=col(L0_ffn_ln2_weight), ln2b=col(L0_ffn_ln2_bias),
        wqkv=own(np.asarray(L0_ffn_qkv_weight).T), wproj=own(np.asarray(L0_ffn_proj_weight).T),
        wrouter=np.asarray(L0_ffn_router_weight), w1=np.asarray(L0_ffn_moe_w1), w2=np.asarray(L0_ffn_moe_w2),
        cos=table(np.cos(angle), np.cos(angle)), sin=table(-np.sin(angle), np.sin(angle)),
        identf=np.eye(P, dtype=np.float32), ones1=np.ones((1, P), np.float32),
        tri=np.triu(np.ones((P, P), np.float32), 1).astype(bf16), allones=np.ones((P, P), bf16),
        rev8=np.tile(np.arange(E, 0, -1, dtype=np.float32), (P, 1)),
        ebase=np.tile(np.arange(E, dtype=np.float32) * CAP, (P, 1)),
        dump=(SLOTS + TOPK * token + np.arange(TOPK)[None, :, None]).reshape(P, -1).astype(np.float32),
    )
    nc = bacc.Bacc("TRN2", target_bir_lowering=False, num_devices=1)
    aps = {n: nc.dram_tensor(f"in_{n}", a.shape, mybir.dt.from_np(a.dtype), kind="ExternalInput").ap() for n, a in arrays.items()}
    out = nc.dram_tensor("out", (S, T, D), F32, kind="ExternalOutput").ap()
    build(nc, **aps, out=out)
    r = run_bass_kernel_spmd(nc, [{f"in_{n}": a for n, a in arrays.items()}], core_ids=[0])
    return r.results[0]["out"]
```

```python
from contextlib import ExitStack

import numpy as np

import concourse.bass as bass
from concourse import mybir

F32 = mybir.dt.float32
BF16 = mybir.dt.bfloat16
U32 = mybir.dt.uint32
ALU = mybir.AluOpType
ACT = mybir.ActivationFunctionType
AX_X = mybir.AxisListType.X

P = 128
S, T, D = 8, 512, 128
TT = T // P
NT = S * TT
H, HD = 16, 8
LAT = 32
G, QH = 4, 4
GW = (QH + 2) * HD
QKV = G * GW
E, FF, TOPK = 8, 256, 2
FH = FF // P
CAP = int(np.ceil(S * T * TOPK / E * 1.25))
CT = CAP // P
SLOTS = E * CAP
HALVES = NT * E // P
EPS = 1e-5
SCALE = float(1.0 / np.sqrt(np.float32(HD)))
NEG = -3.0e38
CHUNK = S // 2
LOOP = range(4, 7)
HELPED_QK = [2, 1, 0, 0] + [2] * len(LOOP) + [0]
HELPED_PV = [0, 0, 2, 2, 2, 2, 0, 0]
SUMMED_QK, QK_TILES = (0, 1, 2, 3, 7), 2
SUMMED_PV = [2, 4, 1, 1, 1, 1, 4, 3]
FEW_IN = [s for s in range(S) if SUMMED_PV[s] < TT]
EARLY = S - 2
OWN_NORM = TT // 2
OWN_KEYS = range(3)
BANKS = 4


def build(nc, x, wq, bq, wdown, bdown, wupk, wupv, wout, bout, ln1w, ln1b, ln2w, ln2b,
          wqkv, wproj, wrouter, w1, w2, cos, sin, identf, ones1, tri, allones, rev8, ebase, dump, earlier, out):
    slots_d = nc.dram_tensor("slot_rows", (SLOTS + S * T * TOPK, D), F32, kind="Internal").ap()
    expert_d = nc.dram_tensor("expert_rows", (SLOTS, D), F32, kind="Internal").ap()

    with ExitStack() as ctx:
        def sb(name, shape, dt=F32):
            return ctx.enter_context(nc.sbuf_tensor(name, shape, dt))

        def ps(name, shape, dt=F32):
            return ctx.enter_context(nc.psum_tensor(name, shape, dt))

        def sem(name):
            return ctx.enter_context(nc.semaphore(name))

        def room(of, at, *shape):
            n = int(np.prod(shape))
            names = [f"a{k}" for k in range(len(shape))]
            return of[:, at:at + n].rearrange(f"p ({' '.join(names)}) -> p {' '.join(names)}", **dict(zip(names, shape)))

        given = dict(identf=identf, ln1w=ln1w, ln1b=ln1b, wqkv=wqkv, wdown=wdown, bdown=bdown, wq=wq, bq=bq, ones1=ones1,
                     wupk=wupk, wupv=wupv, cos=cos, sin=sin, wproj=wproj, ln2w=ln2w, ln2b=ln2b, wrouter=wrouter,
                     wout=wout, bout=bout.partition_broadcast(P), rev8=rev8, ebase=ebase, dump=dump, tri=tri, allones=allones, earlier=earlier)
        sizes = dict(identf=[P, P], ln1w=[P, 1], ln1b=[P, 1], wqkv=[P, QKV], wdown=[P, LAT], bdown=[LAT, 1], wq=[P, D], bq=[1, D],
                     ones1=[1, P], wupk=[LAT + 1, D], wupv=[LAT + 1, D], cos=[P, TT * D], sin=[P, TT * D], wproj=[P, D],
                     ln2w=[P, 1], ln2b=[P, 1], wrouter=[P, E], wout=[P, D], bout=[P, D], rev8=[P, E], ebase=[P, E],
                     dump=[P, TOPK * NT], tri=[P, P], allones=[P, P], earlier=[P, HALVES * NT * E])
        C = {n: sb("c_" + n, sizes[n], BF16 if n in ("tri", "allones", "earlier") else F32) for n in given}

        xn_all = sb("xn_all", [P, S, TT, D])
        qkv_all = sb("qkv_all", [P, S, TT * QKV])
        qkv_t = qkv_all[:].rearrange("p s (a c) -> p s a c", a=TT)
        z2_all = qkv_all[:, :, 0:TT * D].rearrange("p s (a d) -> p s a d", a=TT)
        q_all = sb("q_all", [P, S, TT * D])
        k_all = sb("k_all", [P, S, TT * D])
        v_all = sb("v_all", [P, S, TT * D])
        prod = sb("prod", [P, 6 * H * H * HD])
        prodA, prodB, prodC = (room(prod, i * 2 * H * H * HD, 2, H * H * HD) for i in range(3))
        zeros = room(prodC[:, 1, :], 0, 1, D)
        score = sb("score", [P, 2, TT * H * H])
        hmax = sb("hmax", [P, 2, TT * H])
        hsum = sb("hsum", [P, 2, TT * H])
        ao = sb("ao", [P, 2, TT, D])
        stat = sb("stat", [P, NT, 6])
        mom = sb("mom", [P, 6, NT])
        eps = sb("eps", [P, 1])

        flat = sb("flat", [P, 8 * CAP])
        zb = room(flat, 0, CHUNK, TT, D)
        xnb = room(flat, 0, 2, TT, D)
        xnT = room(flat, 2048, 2, T)
        lnT = room(flat, 3072, 2, T)
        latT = room(flat, 4096, 2, T)
        aoc = room(flat, 5120, 2, TT, D)
        bT = room(flat, 6144, T)
        t1 = room(flat, 6656, 2, TT * D)
        t2 = room(flat, 7680, 2, TT * D)
        xe = room(flat, 0, 2, CT, D)
        xeT = room(flat, 2 * CAP, CAP)
        hT = room(flat, 3 * CAP, FH, CAP)
        ye = room(flat, 5 * CAP, 2, CT, D)
        w1_sb = room(flat, 7 * CAP, 2, FF)
        w2_sb = room(flat, 7 * CAP + 2 * FF, 2, FH, D)
        yg = room(flat, 0, S, TT, TOPK, D)
        gb = room(flat, 9216, 2, TT, D)
        aoT = sb("aoT", [P, T])

        value_buf = [prodB[:, 0, :], prodB[:, 1, :], prodC[:, 0, :], prodC[:, 1, :]]
        past = room(qkv_all[:].rearrange("p s c -> p (s c)"), 0, 2, H * H * HD)
        late = room(qkv_all[:].rearrange("p s c -> p (s c)"), 2 * H * H * HD, 4, TT * D)
        turned_buf = ((t1[:, 0], t1[:, 1]), (t2[:, 0], t2[:, 1]))
        late_buf = ((late[:, 0], late[:, 1]), (late[:, 2], late[:, 3]))
        help_buf = {0: {2: value_buf[0], 3: value_buf[1]}, 1: {3: value_buf[2]}}
        help_buf.update({s: {2: past[:, 0], 3: past[:, 1]} for s in range(2, S)})
        xr = prodA.rearrange("p l (s a d) -> p (l s) a d", a=TT, d=D)

        UNIT = S * (S + 1) // 2 * QH * HD

        def from_key(kind, par, t):
            first = (t * S - t * (t - 1) // 2) * QH * HD
            return room(prod, (2 * kind + par) * 2 * UNIT, 2, UNIT)[:, :, first:first + (S - t) * QH * HD]

        sc = score[:, 0, 0:2 * S * S * QH].rearrange("p (l t s q) -> p l t s q", l=2, t=S, s=S)
        sc2 = score[:, 0, 2 * S * S * QH:].rearrange("p (l t s q) -> p l t s q", l=2, t=S, s=S)
        smax = hmax[:, 0, :].rearrange("p (l m) -> p l m", l=2)
        ssum = hsum[:, 0, :].rearrange("p (l m) -> p l m", l=2)

        logit = sb("logit", [P, NT, E])
        best = sb("best", [P, TOPK, NT])
        kept = room(prodC[:, 1, :], 0, TOPK, NT, E)
        place = room(prodC[:, 1, :], 2 * NT * E, NT, E)
        onehot = room(prodC[:, 1, :], 3 * NT * E, TOPK, NT, E)
        fits = room(prodC[:, 1, :], 5 * NT * E, NT, E)
        placed = room(prodC[:, 1, :], 6 * NT * E, TOPK, NT, E)
        tmp8 = place
        tmp1 = sb("tmp1", [P, NT])
        fit = sb("fit", [P, TOPK, NT])
        other = sb("other", [P, TOPK, NT])
        behind = sb("behind", [P, TOPK, NT])
        gate = sb("gate", [P, TOPK, NT])
        gate_s = sb("gate_s", [P, 2, TOPK, TT])
        tot16 = sb("tot16", [P, NT * E], BF16)
        mask16 = sb("mask16", [P, NT, E], BF16)
        gather_at = sb("gather_at", [P, TOPK, NT], U32)
        scatter_at = sb("scatter_at", [P, TOPK, NT], U32)

        bank = [ps(f"bank{i}", [P, T]) for i in range(8)]

        names = """consts_in filled
            moments norm1 norm1_part dev_done xnb_done zb_done zb_part xnT_ready xnT_done zT_ready lnT_done lat_ready lat_done
            bqkv_ready bqkv_done q_ready k_ready k_done v_ready v_done q_done turn_step turned own_turn own_turned own_qk
            qk_prod qk_score s_max s_diff s_exp s_sum s_rsum s_prob pv_own pv_prod pv_ready block_kept
            aoc_done bT_ready bT_done proj_ready h1_done z2_done z2_part z2T_ready x2T_done logit_ready logit_kept
            route diff_done route_exp mask_done tot_ready tot_kept pos_ready index_done zero_done zero_out scattered
            prod_done sum_done score_sum help_qk score_done row_max row_diff row_exp row_sum row_inv
            help_pv value_prod value_part value_sum ao_done ao_ready aoT_done attn_ready attn_done
            part_ready part_kept
            tail_in gate_in f_step silu_done gate_done res_done""".split()
        W = {n: sem(n) for n in names}
        x_in, w_in, ye_out, gathered, y_out = ([sem(f"{n}{i}") for i in range(2)] for n in ("x_in", "w_in", "ye_out", "gathered", "y_out"))
        xe_in = [sem(f"xe_in{i}") for i in range(2 * 3)]
        block = ctx.enter_context(nc.Block())

        def ev(half, par):
            return 2 * half + par

        def after(half, par):
            return (half, 1) if par == 0 else (half + 1, 0)

        def wait_past(eng, name, count):
            if not isinstance(count, int) or count > 0:
                eng.wait_ge(W[name] if isinstance(name, str) else name, count)

        def staggered(eng, first, second):
            first(0, 0, False)
            first(0, 1, False)
            second(0, 0, False)
            first(1, 0, True)
            second(0, 1, False)
            with eng.Fori(1, S // 2 - 1) as half:
                for par in range(2):
                    first(*after(half, par), True)
                    second(half, par, True)
            first(S // 2 - 1, 1, True)
            second(S // 2 - 1, 0, True)
            second(S // 2 - 1, 1, True)

        def in_pairs(eng, body, last=S):
            body(0, 0, False)
            body(0, 1, False)
            with eng.Fori(1, last // 2) as half:
                for par in range(2):
                    body(half, par, True)

        n_consts = 16 * len(given)
        chunks = [(i, min(T, CAP - i)) for i in range(0, CAP, T)]

        assert len(chunks) == 3
        PARTS = 3 + 3 * FH + 3

        def fourth(eng, first, expert, attention):
            def with_experts(half, par):
                first(half + 2, par)
                expert(half, 0)
                expert(half, 1)
                attention(half + 2, par)

            for s in (0, 1):
                first(s, s)
                attention(s, s)
            with_experts(0, 0)
            with eng.Fori(0, E // 4 - 1) as j:
                with_experts(2 * j + 1, 1)
                with_experts(2 * j + 2, 0)
            with_experts(E // 2 - 1, 1)
            for s in (S - 2, S - 1):
                first(s, s % 2)
                attention(s, s % 2)

        def few(s):
            return SUMMED_PV[s if isinstance(s, int) else 3]

        def counted(s, of_batch):
            if isinstance(s, int):
                return sum(of_batch(i) for i in range(s))
            each = of_batch(LOOP.start)
            return each * s + (counted(LOOP.start, of_batch) - each * LOOP.start)

        helped_qk = lambda i: HELPED_QK[i]
        own_qk = lambda i: TT - HELPED_QK[i]
        vector_sums = lambda i: TT - 1 - (QK_TILES if i in SUMMED_QK else 0)

        def eager(s):
            return not isinstance(s, int) or (s > 0 and few(s - 1) <= few(s) < TT)

        def value_plan(s):
            own = TT - HELPED_PV[s if isinstance(s, int) else 3]
            return own, few(s), [*range(few(s), own), *range(few(s))] if eager(s) else [*range(own)]

        def few_before(s):
            before = lambda s: len([i for i in FEW_IN if i < s])
            return before(s) if isinstance(s, int) else s - 3 + before(3)

        helped_pv = lambda i: HELPED_PV[i]
        own_pv = lambda i: TT - HELPED_PV[i]

        def key_product(eng, half, par, lg, keys):
            at = (2 * par + lg) * GW
            for t in keys:
                i = eng.tensor_tensor(from_key(0, par, t)[:, lg].rearrange("p (s q d) -> p s q d", q=QH, d=HD),
                                      qkv_t[:, t:S, half, at:at + QH * HD].rearrange("p s (q d) -> p s q d", d=HD),
                                      qkv_t[:, t, half, at + QH * HD:at + (QH + 1) * HD].unsqueeze(1).unsqueeze(1)
                                      .broadcast_to([P, S - t, QH, HD]), ALU.mult)
            return i

        def value_products(eng, half, par, lg):
            at = (2 * par + lg) * GW + (QH + 1) * HD
            for t in range(S):
                i = eng.tensor_tensor(from_key(1, par, t)[:, lg].rearrange("p (s q d) -> p s q d", q=QH, d=HD),
                                      sc2[:, lg, t, t:S, :].unsqueeze(3).broadcast_to([P, S - t, QH, HD]),
                                      qkv_t[:, t, half, at:at + HD].unsqueeze(1).unsqueeze(1).broadcast_to([P, S - t, QH, HD]), ALU.mult)
            return i

        def qk_product(eng, dst, s, sp, a):
            at = slice(a * D, (a + 1) * D)
            return eng.tensor_tensor(dst.rearrange("p (h g d) -> p h g d", h=H, g=H),
                                     q_all[:, s, at].rearrange("p (h d) -> p h d", d=HD).unsqueeze(2).broadcast_to([P, H, H, HD]),
                                     k_all[:, s, at].rearrange("p (g d) -> p g d", d=HD).unsqueeze(1).broadcast_to([P, H, H, HD]), ALU.mult)

        def turn(eng, v, s, with_cos, with_sin):
            halves = lambda v: v.rearrange("p (m two f) -> p m two f", two=2, f=HD // 2)
            eng.tensor_tensor(with_cos, v[:, s, :], C["cos"][:], ALU.mult)
            for own, other in ((0, 1), (1, 0)):
                i = eng.tensor_tensor(halves(with_sin)[:, :, own, :], halves(v[:, s, :])[:, :, other, :], halves(C["sin"][:])[:, :, own, :], ALU.mult)
            return i

        def qk_product_wide(eng, dst, s, sp, a):
            at = slice(a * D, (a + 1) * D)
            return eng.tensor_tensor(dst.rearrange("p (d h g) -> p d h g", h=H, g=H),
                                     q_all[:, s, at].rearrange("p (h d) -> p d h", d=HD).unsqueeze(3).broadcast_to([P, HD, H, H]),
                                     k_all[:, s, at].rearrange("p (g d) -> p d g", d=HD).unsqueeze(2).broadcast_to([P, HD, H, H]), ALU.mult)

        def pv_product(eng, s, sp, a):
            return eng.tensor_tensor(value_buf[a].rearrange("p (g h d) -> p g h d", g=H, h=H),
                                     score[:, sp, a * H * H:(a + 1) * H * H].rearrange("p (h g) -> p g h", g=H).unsqueeze(3)
                                     .broadcast_to([P, H, H, HD]),
                                     v_all[:, s, a * D:(a + 1) * D].rearrange("p (d g) -> p g d", g=H).unsqueeze(2)
                                     .broadcast_to([P, H, H, HD]), ALU.mult)

        @block.sync
        def _(sp):
            for s in range(S):
                sp.dma_start(xn_all[:, s], x[s].rearrange("(a p) d -> p a d", p=P)).then_inc(x_in[s // CHUNK], 16)
            for n, src in given.items():
                sp.dma_start(C[n][:], src).then_inc(W["consts_in"], 16)
            sp.wait_ge(W["zero_done"], 1)
            for k in range(CT):
                sp.dma_start(slots_d[k * E * P:(k + 1) * E * P, :].rearrange("(p a) d -> p a d", p=P),
                             zeros.broadcast_to([P, E, D])).then_inc(W["zero_out"], 16)

            def load_weights(half, par):
                e = ev(half, par)
                sp.dma_start(w1_sb[:, par], w1[e]).then_inc(w_in[par], 16)
                sp.dma_start(w2_sb[:, par], w2[e].rearrange("(f p) d -> p f d", p=P)).then_inc(w_in[par], 16)

            def load_rows(half, par):
                for q, (at, n) in enumerate(chunks):
                    sp.dma_start(xe[:, par, at // P:(at + n) // P], slots_d[bass.ds(ev(half, par) * CAP + at, n), :]
                                 .rearrange("(a p) d -> p a d", p=P)).then_inc(xe_in[3 * par + q], 16)

            def store(half, par):
                e = ev(half, par)
                for q, (at, n) in enumerate(chunks):
                    sp.wait_ge(W["part_kept"], PARTS * e + 3 + 3 * FH + q + 1)
                    sp.dma_start(expert_d[bass.ds(e * CAP + at, n), :].rearrange("(a p) d -> p a d", p=P),
                                 ye[:, par, at // P:(at + n) // P]).then_inc(ye_out[par], 16)

            load_weights(0, 0)
            load_weights(0, 1)
            sp.wait_ge(W["index_done"], 1)
            sp.wait_ge(W["z2_part"], S)
            sp.wait_ge(W["turned"], 2 * (EARLY - 1))
            sp.wait_ge(W["v_ready"], S)
            sp.wait_ge(W["q_ready"], S)
            sp.wait_ge(W["scattered"], 16 * NT * TOPK)
            load_rows(0, 0)
            load_rows(0, 1)
            with sp.Fori(0, E // 2 - 1) as half:
                for par in range(2):
                    store(half, par)
                    load_weights(half + 1, par)
                    load_rows(half + 1, par)
            store(E // 2 - 1, 0)
            store(E // 2 - 1, 1)

            sp.wait_ge(W["score_done"], S)
            sp.wait_ge(W["score_sum"], QK_TILES * len(SUMMED_QK))
            sp.dma_start(xr, x.rearrange("s (a p) d -> p (s a) d", p=P).rearrange("p (s a) d -> p s a d", a=TT)).then_inc(W["tail_in"], 16)
            with sp.Fori(0, S // 2) as half:
                for par in range(2):
                    s = ev(half, par)
                    sp.wait_ge(W["res_done"], s + 1)
                    sp.dma_start(out[s].rearrange("(a p) d -> p a d", p=P), xr[:, s]).then_inc(y_out[par], 16)
            for par in range(2):
                sp.wait_ge(y_out[par], 16 * (S // 2))

        @block.vector
        def _(dve):
            V = nc.vector
            V.memset(zeros, 0.0).then_inc(W["zero_done"], 1)
            V.memset(eps[:], EPS)
            V.memset(latT[LAT:LAT + 1], 1.0)
            V.memset(sc, NEG).then_inc(W["filled"], 1)

            count = {"moments": 0, "route": 0}

            def link(name, ins):
                ins.then_inc(W[name], 1)
                count[name] += 1
                dve.wait_ge(W[name], count[name])

            def statistics(first, last):
                for s in range(first, last):
                    for a in range(TT):
                        i = V.bn_stats(stat[:, s * TT + a, :], xn_all[:, s, a, :])
                    i.then_inc(W["moments"], 1)
                count["moments"] += last - first
                dve.wait_ge(W["moments"], count["moments"])

            def deviations(first, last, row, devs):
                J = slice(first * TT, last * TT)
                even, odd = stat[:, J, 1], stat[:, J, 4]
                mean, inv, dif, sq = (mom[:, r, J] for r in (row, row + 1, 4, 5))
                V.tensor_tensor(mean, even, odd, ALU.add)
                V.tensor_tensor(dif, even, odd, ALU.subtract)
                link("moments", V.tensor_tensor(sq, stat[:, J, 2], stat[:, J, 5], ALU.add))
                V.tensor_scalar(mean, mean, 0.5, None, ALU.mult)
                link("moments", V.tensor_tensor(dif, dif, dif, ALU.mult))
                V.scalar_tensor_tensor(inv, dif, float(D // 4), sq, ALU.mult, ALU.add).then_inc(W["moments"], 1)
                count["moments"] += 1
                dve.wait_ge(W["dev_done"], devs)
                link("moments", V.reciprocal(inv, inv))
                link("moments", V.scalar_tensor_tensor(dif, mean, -1.0, inv, ALU.mult, ALU.mult))

            def normalized(dst, s, row):
                for a in range(OWN_NORM):
                    n = s * TT + a
                    i = V.tensor_scalar(dst[:, a, :], xn_all[:, s, a, :], mom[:, row, n:n + 1], mom[:, row + 1, n:n + 1], ALU.subtract, ALU.mult)
                return i

            for c in range(2):
                first, last = c * CHUNK, (c + 1) * CHUNK
                dve.wait_ge(x_in[c], 16 * CHUNK)
                statistics(first, last)
                deviations(first, last, 0, 2 * c + 1)
                for s in range(first, last):
                    normalized(xn_all[:, s], s, 0).then_inc(W["norm1"], 1)
                dve.wait_ge(W["norm1"], last)
                dve.wait_ge(W["norm1_part"], last)
                statistics(first, last)
                deviations(first, last, 2, 2 * c + 2)
                for s in range(first, last):
                    if s >= CHUNK:
                        dve.wait_ge(W["zT_ready"], s - CHUNK + 1)
                    normalized(zb[:, s % CHUNK], s, 2).then_inc(W["zb_done"], 1)


            def unit(half, par, steady):
                u = ev(half, par)
                key_product(V, half, par, 0, range(S) if not steady and not par else OWN_KEYS).then_inc(W["own_qk"], 1)
                dve.wait_ge(W["own_qk"], u + 1)
                some = steady or par
                dve.wait_ge(W["qk_prod"], u + 1)
                for t in range(S):
                    i = V.tensor_reduce(sc[:, :, t, t:S, :].rearrange("p l s q -> p l (s q)"), from_key(0, par, t).rearrange("p l (m d) -> p l m d", d=HD),
                                        AX_X, ALU.add)
                i.then_inc(W["qk_score"], 1)
                dve.wait_ge(W["qk_score"], u + 1)
                V.tensor_reduce(smax, sc.rearrange("p l t s q -> p l (s q) t"), AX_X, ALU.max).then_inc(W["s_max"], 1)
                dve.wait_ge(W["s_max"], u + 1)
                if some:
                    wait_past(dve, "pv_prod", u)
                V.tensor_tensor(sc2.rearrange("p l t s q -> p l t (s q)"), sc.rearrange("p l t s q -> p l t (s q)"),
                                smax.unsqueeze(2).broadcast_to([P, 2, S, S * QH]), ALU.subtract).then_inc(W["s_diff"], 1)
                dve.wait_ge(W["s_exp"], u + 1)
                V.tensor_reduce(ssum, sc2.rearrange("p l t s q -> p l (s q) t"), AX_X, ALU.add).then_inc(W["s_sum"], 1)
                dve.wait_ge(W["s_sum"], u + 1)
                V.reciprocal(ssum, ssum).then_inc(W["s_rsum"], 1)
                dve.wait_ge(W["s_rsum"], u + 1)
                V.tensor_tensor(sc2.rearrange("p l t s q -> p l t (s q)"), sc2.rearrange("p l t s q -> p l t (s q)"),
                                ssum.unsqueeze(2).broadcast_to([P, 2, S, S * QH]), ALU.mult).then_inc(W["s_prob"], 1)
                if steady:
                    dve.wait_ge(W["pv_ready"], u - 1)
                dve.wait_ge(W["s_prob"], u + 1)
                value_products(V, half, par, 0).then_inc(W["pv_own"], 1)

            dve.wait_ge(W["bqkv_done"], S)
            in_pairs(dve, unit)

            dve.wait_ge(W["q_done"], 1)
            dve.wait_ge(W["k_done"], 1)
            dve.wait_ge(W["qk_score"], S)
            dve.wait_ge(W["zero_out"], 16 * CT)
            for i, v in enumerate((k_all, q_all)):
                with_cos, with_sin = (prodC[:, 1, (2 * i + j) * TT * D:(2 * i + j + 1) * TT * D] for j in range(2))
                turn(V, v, 0, with_cos, with_sin).then_inc(W["own_turn"], 1)
            for i, v in enumerate((k_all, q_all)):
                dve.wait_ge(W["own_turn"], 2)
                with_cos, with_sin = (prodC[:, 1, (2 * i + j) * TT * D:(2 * i + j + 1) * TT * D] for j in range(2))
                V.tensor_tensor(v[:, 0, :], with_cos, with_sin, ALU.add).then_inc(W["own_turned"], 1)
            dve.wait_ge(W["own_turned"], 2)
            for a in range(QK_TILES):
                qk_product_wide(V, prodA[:, a, :], 0, 0, a).then_inc(W["prod_done"], 1)
            def residual(half, par, steady):
                s = ev(half, par)
                dve.wait_ge(W["proj_ready"], s + 1)
                V.tensor_tensor(xn_all[:, s], bank[2 + par][:].rearrange("p (a d) -> p a d", a=TT), xn_all[:, s], ALU.add).then_inc(W["h1_done"], 1)
                dve.wait_ge(W["h1_done"], s + 1)
                for a in range(TT):
                    i = V.bn_stats(stat[:, s * TT + a, :], xn_all[:, s, a, :])
                i.then_inc(W["moments"], 1)

            in_pairs(dve, residual)
            count["moments"] += S
            dve.wait_ge(W["moments"], count["moments"])
            deviations(0, S, 0, 5)

            for s in range(S):
                normalized(z2_all[:, s], s, 0).then_inc(W["z2_done"], 1)
            def total(s, sp, a):
                own = TT - HELPED_QK[s if isinstance(s, int) else LOOP.start]
                dve.wait_ge(W["help_qk"], counted(s, helped_qk) + a - own + 1)
                i = V.tensor_reduce(score[:, sp, a * H * H:(a + 1) * H * H], help_buf[s if isinstance(s, int) else LOOP.start][a]
                                    .rearrange("p (m d) -> p m d", d=HD), AX_X, ALU.add)
                i.then_inc(W["score_done" if a == TT - 1 else "sum_done"], 1)

            def scores(s, sp):
                kind = s if isinstance(s, int) else LOOP.start
                summed = QK_TILES if kind in SUMMED_QK else 0
                own = TT - HELPED_QK[kind]
                order = [a for a in ((0, 2, 1, 3) if summed else (0, 1, 2, 3)) if a < own]
                buf = {0: 0, 1: 1, 2: 1, 3: 0}
                assert summed or own <= 2
                sums = counted(s, vector_sums)

                def product(a):
                    (qk_product_wide if a < summed else qk_product)(V, prodA[:, buf[a], :], s, sp, a).then_inc(W["prod_done"], 1)

                def own_total(a):
                    dve.wait_ge(W["prod_done"], counted(s, own_qk) + order.index(a) + 1)
                    i = V.tensor_reduce(score[:, sp, a * H * H:(a + 1) * H * H], prodA[:, buf[a], :].rearrange("p (m d) -> p m d", d=HD), AX_X, ALU.add)
                    i.then_inc(W["score_done" if a == TT - 1 else "sum_done"], 1)

                if isinstance(s, int):
                    dve.wait_ge(W["turned"], 2 * s if s == 1 or s >= EARLY else 2 * (EARLY - 1))
                dve.wait_ge(W["sum_done"], sums)
                dve.wait_ge(W["score_done"], s)
                if kind - 1 in SUMMED_QK:
                    dve.wait_ge(W["score_sum"], QK_TILES * len([i for i in SUMMED_QK if i < kind]))
                product(0)
                if summed and own > 2:
                    product(2)
                    own_total(2)
                    dve.wait_ge(W["sum_done"], sums + 1)
                    product(1)
                    if own > 3:
                        dve.wait_ge(W["score_sum"], QK_TILES * SUMMED_QK.index(kind) + 1)
                        product(3)
                        own_total(3)
                    else:
                        total(s, sp, 3)
                else:
                    product(1)
                    for a in range(summed, TT):
                        own_total(a) if a < own else total(s, sp, a)

            rows = lambda v: v.rearrange("p (m g) -> p m g", g=H)

            def differences(par, s):
                later = lambda n: not isinstance(s, int) or s >= n
                dve.wait_ge(W["score_done"], s + 1)
                n = QK_TILES if isinstance(s, int) and s in SUMMED_QK else 0
                if n:
                    dve.wait_ge(W["score_sum"], QK_TILES * (SUMMED_QK.index(s) + 1))
                parts = [(rows(bank[5][:, 0:n * H * H]), 0, n)] * (n > 0) + [(rows(score[:, par, n * H * H:]), n, TT)]
                for src, a, b in parts:
                    i = V.tensor_reduce(hmax[:, par, a * H:b * H], src, AX_X, ALU.max)
                i.then_inc(W["row_max"], 1)
                dve.wait_ge(W["row_max"], s + 1)
                for src, a, b in parts:
                    i = V.tensor_tensor(rows(score[:, par, a * H * H:b * H * H]), src,
                                        hmax[:, par, a * H:b * H].unsqueeze(2).broadcast_to([P, (b - a) * H, H]), ALU.subtract)
                i.then_inc(W["row_diff"], 1)
                if not isinstance(s, int) or s + 1 < S:
                    if later(1):
                        dve.wait_ge(W["value_prod"], counted(s, own_pv))
                    if later(3):
                        dve.wait_ge(W["help_pv"], counted(s, helped_pv))
                    scores(s + 1, 1 - par)

            for a in range(TT - HELPED_QK[0], TT):
                total(0, 0, a)
            differences(0, 0)

            dve.wait_ge(W["logit_ready"], S)
            V.tensor_copy(logit[:].rearrange("p n e -> p (n e)"), bank[6][:, 0:NT * E]).then_inc(W["logit_kept"], 1)

            def step(ins):
                link("route", ins)

            lg = logit[:]
            full = lambda v: v[:].unsqueeze(2).broadcast_to([P, NT, E])
            each = lambda v: v[:].unsqueeze(1).broadcast_to([P, NT, E])
            dve.wait_ge(W["logit_kept"], 1)
            for k in range(TOPK):
                step(V.tensor_reduce(best[:, k, :], lg, AX_X, ALU.max))
                step(V.tensor_tensor(tmp8, lg, best[:, k, :].unsqueeze(2).broadcast_to([P, NT, E]), ALU.is_equal))
                step(V.tensor_tensor(tmp8, tmp8, each(C["rev8"]), ALU.mult))
                step(V.tensor_reduce(tmp1[:], tmp8, AX_X, ALU.max))
                step(V.tensor_tensor(onehot[:, k], tmp8, full(tmp1), ALU.is_equal))
                if k == 0:
                    step(V.scalar_tensor_tensor(lg, onehot[:, 0], NEG, lg, ALU.mult, ALU.add))
            V.tensor_tensor(mask16[:], onehot[:, 0], onehot[:, 1], ALU.add).then_inc(W["mask_done"], 1)
            V.tensor_tensor(tmp1[:], best[:, 1, :], best[:, 0, :], ALU.subtract).then_inc(W["diff_done"], 1)
            dve.wait_ge(W["route_exp"], 1)
            step(V.tensor_scalar(tmp1[:], gate[:, 1, :], 1.0, None, ALU.add))
            step(V.reciprocal(gate[:, 0, :], tmp1[:]))
            step(V.tensor_tensor(gate[:, 1, :], gate[:, 1, :], gate[:, 0, :], ALU.mult))
            dve.wait_ge(W["pos_ready"], 1)
            pos = bank[0][:, 0:NT * E].rearrange("p (n e) -> p n e", e=E)
            flat_ne = lambda v: v.rearrange("p k n e -> p k (n e)")
            both = lambda v: v.rearrange("p n e -> p (n e)").unsqueeze(1).broadcast_to([P, TOPK, NT * E])
            dump_row = C["dump"][:].rearrange("p (k n) -> p k n", k=TOPK)
            V.tensor_scalar(fits, pos, float(CAP), None, ALU.is_lt)
            step(V.tensor_tensor(place, pos, each(C["ebase"]), ALU.add))
            step(V.tensor_tensor(flat_ne(kept), flat_ne(onehot), both(fits), ALU.mult))
            V.tensor_reduce(fit[:], kept, AX_X, ALU.add)
            step(V.tensor_tensor(flat_ne(placed), flat_ne(kept), both(place), ALU.mult))
            V.tensor_reduce(best[:], placed, AX_X, ALU.add)
            step(V.tensor_tensor(other[:], fit[:], dump_row, ALU.mult))
            V.tensor_copy(gather_at[:], best[:])
            step(V.tensor_tensor(behind[:], best[:], dump_row, ALU.add))
            step(V.tensor_tensor(behind[:], behind[:], other[:], ALU.subtract))
            V.tensor_copy(scatter_at[:], behind[:]).then_inc(W["index_done"], 1)
            step(V.tensor_tensor(gate[:], gate[:], fit[:], ALU.mult))

            def combine(half, par, steady):
                s = ev(half, par)
                h1 = xn_all[:, s]
                if steady:
                    dve.wait_ge(W["f_step"], 2 * s - 2)
                V.tensor_copy(gate_s[:, par], gate[:].rearrange("p k (s a) -> p k s a", a=TT)[:, :, s, :]).then_inc(W["gate_in"], 1)
                dve.wait_ge(W["gate_in"], s + 1)
                dve.wait_ge(gathered[par], 16 * TT * TOPK * (half + 1))
                for k in range(TOPK):
                    for a in range(TT):
                        i = V.scalar_tensor_tensor(h1[:, a, :], yg[:, s, a, k, :], gate_s[:, par, k, a:a + 1], h1[:, a, :], ALU.mult, ALU.add)
                    i.then_inc(W["f_step"], 1)
                    dve.wait_ge(W["f_step"], TOPK * s + k + 1)

            def normalize(s, par):
                dve.wait_ge(W["value_sum"], s + 1)
                if few(s) < TT:
                    dve.wait_ge(W["value_part"], few_before(s) + 1)
                if not isinstance(s, int) or s >= 2:
                    dve.wait_ge(W["ao_ready"], s - 1)
                tiles = few(s)
                for src, a, b in ((bank[7][:].rearrange("p (a d) -> p a d", d=D), 0, tiles), (ao[:, par], tiles, TT)):
                    if b > a:
                        i = V.tensor_tensor(ao[:, par, a:b].rearrange("p a (h d) -> p (a h) d", d=HD),
                                            src[:, a:b].rearrange("p a (h d) -> p (a h) d", d=HD),
                                            hsum[:, par, a * H:b * H].unsqueeze(2).broadcast_to([P, (b - a) * H, HD]), ALU.mult)
                i.then_inc(W["ao_done"], 1)

            def branch_out(s):
                dve.wait_ge(W["attn_ready"], s + 1)
                V.tensor_tensor(q_all[:, s, :].rearrange("p (a d) -> p a d", a=TT), bank[4][:].rearrange("p (a d) -> p a d", a=TT),
                                C["bout"][:].unsqueeze(1).broadcast_to([P, TT, D]), ALU.add).then_inc(W["attn_done"], 1)

            def values(par, s):
                later = lambda n: not isinstance(s, int) or s >= n
                own, summed, order = value_plan(s)

                def before():
                    if later(2):
                        branch_out(s - 2)
                    if later(1):
                        normalize(s - 1, 1 - par)

                if not eager(s):
                    before()
                dve.wait_ge(W["row_exp"], s + 1)
                if later(3):
                    dve.wait_ge(W["ao_done"], s - 1)
                V.tensor_reduce(hsum[:, par, :], rows(score[:, par]), AX_X, ALU.add).then_inc(W["row_sum"], 1)
                dve.wait_ge(W["row_sum"], s + 1)
                V.reciprocal(hsum[:, par, :], hsum[:, par, :]).then_inc(W["row_inv"], 1)
                if not later(1):
                    dve.wait_ge(W["score_done"], 2)
                elif not eager(s):
                    dve.wait_ge(W["value_sum"], s)
                if not later(3):
                    dve.wait_ge(W["v_done"], s + 1 if s < 2 else S)
                if later(1):
                    wait_past(dve, "value_part", few_before(s))
                for a in order:
                    if a == 0 and eager(s):
                        before()
                    pv_product(V, s, par, a).then_inc(W["value_prod"], 1)
                    if a == own - 1 and summed < TT:
                        if later(2):
                            dve.wait_ge(W["ao_ready"], s - 1)
                        for b in range(summed, TT):
                            if b < own:
                                dve.wait_ge(W["value_prod"], counted(s, own_pv) + order.index(b) + 1)
                            else:
                                dve.wait_ge(W["help_pv"], counted(s, helped_pv) + b - own + 1)
                            i = V.tensor_reduce(ao[:, par, b, :], value_buf[b].rearrange("p (g m) -> p m g", g=H), AX_X, ALU.add)
                        i.then_inc(W["value_part"], 1)
                dve.wait_ge(W["row_inv"], s + 1)

            def batch(par, s):
                differences(par, s)
                values(par, s)

            values(0, 0)
            for s in (1, 2):
                batch(s % 2, s)
            with dve.Fori(1, S // 2 - 2) as half:
                for par in (1, 0):
                    batch(par, 2 * half + 2 - par)
            for s in (S - 3, S - 2):
                batch(s % 2, s)
            in_pairs(dve, combine, S // 2)
            batch(1, S - 1)

            def gated(half, par):
                s = ev(half, par)
                dve.wait_ge(W["silu_done"], s + 1)
                dve.wait_ge(W["attn_done"], s + 1)
                V.tensor_tensor(gb[:, par], gb[:, par], q_all[:, s, :].rearrange("p (a d) -> p a d", a=TT), ALU.mult).then_inc(W["gate_done"], 1)
                dve.wait_ge(W["gate_done"], s + 1)
                dve.wait_ge(W["tail_in"], 16)
                V.tensor_tensor(xr[:, s], xr[:, s], gb[:, par], ALU.add).then_inc(W["res_done"], 1)

            with dve.Fori(S // 4, S // 2 - 1) as half:
                for par in range(2):
                    combine(half, par, True)
                    gated(2 * half - S // 2 + par, 0)
                    gated(2 * half - S // 2 + par, 1)
            branch_out(S - 2)
            normalize(S - 1, 1)
            combine(S // 2 - 1, 0, True)
            gated(S // 2 - 2, 0)
            gated(S // 2 - 2, 1)
            branch_out(S - 1)
            combine(S // 2 - 1, 1, True)
            gated(S // 2 - 1, 0)
            gated(S // 2 - 1, 1)

        @block.tensor
        def _(pe):
            M = nc.tensor
            pe.wait_ge(W["consts_in"], n_consts)
            pe.wait_ge(W["filled"], 1)

            def transposes(dst, src):
                for a in range(TT):
                    i = M.transpose(dst[:, a * P:(a + 1) * P], src[:, a, :], C["identf"][:])
                return i

            def projected(dst, src, weight, width=D, stop=True):
                for a in range(TT):
                    i = M.matmul(dst[:, a * width:(a + 1) * width], src[:, a * P:(a + 1) * P], weight[:], start=True, stop=stop)
                return i

            def turn(s):
                pe.wait_ge(W["zb_done"], s + 1)
                pe.wait_ge(W["zb_part"], s + 1)
                if s >= 2:
                    pe.wait_ge(W["lnT_done"], s - 1)
                transposes(bank[s % 2], zb[:, s % CHUNK]).then_inc(W["zT_ready"], 1)

            def block_qkv(s):
                pe.wait_ge(W["lnT_done"], s + 1)
                if s >= 2:
                    pe.wait_ge(W["bqkv_done"], s - 1)
                for a in range(TT):
                    i = M.matmul(bank[2 + 2 * (s % 2) + a // 2][:, (a % 2) * QKV:(a % 2 + 1) * QKV], lnT[:, s % 2, a * P:(a + 1) * P],
                                 C["wqkv"][:], start=True, stop=True)
                i.then_inc(W["bqkv_ready"], 1)

            turn(0)
            for s in range(S):
                if s + 1 < S:
                    turn(s + 1)
                block_qkv(s)

            def turn_branch(half, par, steady):
                s = ev(half, par)
                pe.wait_ge(W["xnb_done"], s + 1)
                if steady or par:
                    pe.wait_ge(W["xnT_done"], s)
                transposes(bank[2], xnb[:, par]).then_inc(W["xnT_ready"], 1)

            def project_branch(half, par, steady):
                s = ev(half, par)
                later = steady or par
                pe.wait_ge(W["xnT_done"], s + 1)
                if later:
                    pe.wait_ge(W["lat_done"], s)
                M.matmul(bank[4][0:LAT, :], C["wdown"][:], xnT[:, par, :], start=True, stop=True).then_inc(W["lat_ready"], 1)
                if later:
                    pe.wait_ge(W["q_done"], s)
                for a in range(TT):
                    dst = bank[3][:, a * D:(a + 1) * D]
                    M.matmul(dst, xnT[:, par, a * P:(a + 1) * P], C["wq"][:], start=True, stop=False)
                    i = M.matmul(dst, C["ones1"][:], C["bq"][:], start=False, stop=True)
                i.then_inc(W["q_ready"], 1)
                pe.wait_ge(W["lat_done"], s + 1)
                if later:
                    pe.wait_ge(W["k_done"], s)
                projected(bank[6], latT[0:LAT + 1, par, :], C["wupk"]).then_inc(W["k_ready"], 1)
                if later:
                    pe.wait_ge(W["v_done"], s)
                projected(bank[7], latT[0:LAT + 1, par, :], C["wupv"]).then_inc(W["v_ready"], 1)

            def value_sums(half, par):
                u = ev(half, par)
                pe.wait_ge(W["pv_own"], u + 1)
                pe.wait_ge(W["pv_prod"], u + 1)
                wait_past(pe, "block_kept", u)
                total = bank[1][:].rearrange("p (l s w) -> p l s w", l=2, s=S)
                for t in range(S):
                    i = M.matmul(total[:, :, t:S, :], C["identf"][:], from_key(1, par, t).rearrange("p l (s w) -> p l s w", w=QH * HD),
                                 start=(t == 0), stop=(t == S - 1))
                i.then_inc(W["pv_ready"], 1)

            def second_stage(half, par, steady):
                turn_branch(half, par, steady)
                if steady or par:
                    value_sums(half if par else half - 1, 1 - par)
                project_branch(half, par, steady)

            pe.wait_ge(W["bqkv_done"], S)
            in_pairs(pe, second_stage, EARLY)
            for u in range(EARLY - 1, S):
                value_sums(u // 2, u % 2)

            def turn_block(half, par, steady):
                s = ev(half, par)
                pe.wait_ge(W["aoc_done"], s + 1)
                if steady:
                    pe.wait_ge(W["bT_done"], s - 1)
                transposes(bank[par], aoc[:, par]).then_inc(W["bT_ready"], 1)

            def project_block(half, par, steady):
                s = ev(half, par)
                pe.wait_ge(W["bT_done"], s + 1)
                if steady:
                    pe.wait_ge(W["h1_done"], s - 1)
                projected(bank[2 + par], bT, C["wproj"]).then_inc(W["proj_ready"], 1)

            pe.wait_ge(W["xnT_done"], EARLY)
            pe.wait_ge(W["q_done"], EARLY)
            pe.wait_ge(W["block_kept"], S)
            staggered(pe, turn_block, project_block)
            pe.wait_ge(W["v_done"], EARLY)
            pe.wait_ge(W["k_done"], EARLY)

            def sum_scores(s):
                if s > 0:
                    pe.wait_ge(W["row_diff"], s)
                for a in range(QK_TILES):
                    pe.wait_ge(W["prod_done"], counted(s, own_qk) + 1 + (0 if a == 0 else 1 if own_qk(s) == 2 else 2))
                    for d in range(HD):
                        i = M.matmul(bank[5][:, a * H * H:(a + 1) * H * H], C["identf"][:], prodA[:, a, d * H * H:(d + 1) * H * H],
                                     start=(d == 0), stop=(d == HD - 1))
                    i.then_inc(W["score_sum"], 1)

            sum_scores(0)

            def turn_normed(s):
                pe.wait_ge(W["z2_done"], s + 1)
                pe.wait_ge(W["z2_part"], s + 1)
                if s >= 2:
                    pe.wait_ge(W["x2T_done"], s - 1)
                transposes(bank[4 + 3 * (s % 2)], z2_all[:, s]).then_inc(W["z2T_ready"], 1)

            turn_normed(0)
            for s in range(S):
                if s + 1 < S:
                    turn_normed(s + 1)
                pe.wait_ge(W["x2T_done"], s + 1)
                projected(bank[6][:, s * TT * E:(s + 1) * TT * E], lnT[:, s % 2, :], C["wrouter"], E).then_inc(W["logit_ready"], 1)

            sum_scores(1)
            pe.wait_ge(W["mask_done"], 1)
            mask = mask16[:].rearrange("p n e -> p (n e)")
            for h in range(HALVES):
                i = M.matmul(bank[1][:, h * P:(h + 1) * P], mask[:, h * P:(h + 1) * P], C["allones"][:], start=True, stop=True)
            i.then_inc(W["tot_ready"], 1)
            M.matmul(bank[0][:, 0:NT * E], C["tri"][:], mask, start=True, stop=False)
            pe.wait_ge(W["tot_kept"], 1)
            for h in range(HALVES):
                i = M.matmul(bank[0][:, 0:NT * E], tot16[:, h * P:(h + 1) * P], C["earlier"][:, h * NT * E:(h + 1) * NT * E],
                             start=False, stop=(h == HALVES - 1))
            i.then_inc(W["pos_ready"], 1)
            pe.wait_ge(W["h1_done"], S)
            pe.wait_ge(W["logit_kept"], 1)
            for s in range(EARLY, S):
                turn_branch(s // 2, s % 2, True)
                project_branch(s // 2, s % 2, True)
            pe.wait_ge(W["v_done"], S)
            pe.wait_ge(W["index_done"], 1)

            def expert(half, par):
                e = ev(half, par)

                def free(k):
                    if not isinstance(e, int) or PARTS * e + k >= BANKS:
                        pe.wait_ge(W["part_kept"], PARTS * e + k - BANKS + 1)
                    return bank[k % BANKS]

                for q in range(3):
                    dst = free(q)
                    pe.wait_ge(xe_in[3 * par + q], 16 * (half + 1))
                    for a in range(4 * q, min(4 * q + 4, CT)):
                        i = M.transpose(dst[:, (a % 4) * P:(a % 4 + 1) * P], xe[:, par, a, :], C["identf"][:])
                    i.then_inc(W["part_ready"], 1)
                pe.wait_ge(w_in[par], 32 * (half + 1))
                for f in range(FH):
                    for m, (at, n) in enumerate(chunks):
                        dst = free(3 + 3 * f + m)
                        pe.wait_ge(W["part_kept"], PARTS * e + m + 1)
                        M.matmul(dst[:, 0:n], w1_sb[:, par, f * P:(f + 1) * P], xeT[:, at:at + n],
                                 start=True, stop=True).then_inc(W["part_ready"], 1)
                for q in range(3):
                    dst = free(3 + 3 * FH + q)
                    pe.wait_ge(W["part_kept"], PARTS * e + 3 + 3 * (FH - 1) + q + 1)
                    for a in range(4 * q, min(4 * q + 4, CT)):
                        for f in range(FH):
                            i = M.matmul(dst[:, (a % 4) * P:(a % 4 + 1) * P], hT[:, f, a * P:(a + 1) * P],
                                         w2_sb[:, par, f, :], start=(f == 0), stop=(f == FH - 1))
                    i.then_inc(W["part_ready"], 1)

            def turn_out(s, par):
                pe.wait_ge(W["ao_done"], s + 1)
                wait_past(pe, "attn_done", s)
                transposes(bank[4], ao[:, par]).then_inc(W["ao_ready"], 1)

            def project_out(s):
                pe.wait_ge(W["aoT_done"], s + 1)
                projected(bank[4], aoT, C["wout"]).then_inc(W["attn_ready"], 1)

            def sum_values(s, tiles):
                wait_past(pe, "ao_done", s)
                for a in tiles:
                    own = TT - HELPED_PV[s if isinstance(s, int) else 3]
                    if a >= own:
                        pe.wait_ge(W["help_pv"], counted(s, helped_pv) + a - own + 1)
                    else:
                        pe.wait_ge(W["value_prod"], counted(s, own_pv) + value_plan(s)[2].index(a) + 1)
                    for g in range(H):
                        i = M.matmul(bank[7][:, a * D:(a + 1) * D], C["identf"][:], value_buf[a][:, g * D:(g + 1) * D],
                                     start=(g == 0), stop=(g == H - 1))
                return i

            def attention(s, par):
                later = not isinstance(s, int) or s >= 1
                if later:
                    turn_out(s - 1, 1 - par)
                tiles = range(few(s))
                last = sum_values(s, tiles[:2])
                if later:
                    project_out(s - 1)
                if few(s) > 2:
                    last = sum_values(s, tiles[2:])
                last.then_inc(W["value_sum"], 1)

            def next_scores(s, par):
                if isinstance(s, int) and s > 0 and s + 1 in SUMMED_QK:
                    sum_scores(s + 1)

            fourth(pe, next_scores, expert, attention)
            turn_out(S - 1, 1)
            project_out(S - 1)

        @block.scalar
        def _(act):
            A = nc.scalar

            def deviation(first, last, row, links):
                act.wait_ge(W["moments"], links)
                v = mom[:, row + 1, first * TT:last * TT]
                A.activation(v, v, ACT.Sqrt, bias=eps[:], scale=1.0 / D).then_inc(W["dev_done"], 1)

            NORM = lambda batches: batches + 5

            def normalized(dst, s, row):
                for a in range(OWN_NORM, TT):
                    n = s * TT + a
                    i = A.activation(dst[:, a, :], xn_all[:, s, a, :], ACT.Identity, bias=mom[:, 4, n:n + 1], scale=mom[:, row + 1, n:n + 1])
                return i

            act.wait_ge(W["filled"], 1)

            def root(c, row):
                deviation(c * CHUNK, (c + 1) * CHUNK, row, (2 * c + row // 2) * NORM(CHUNK) + CHUNK + 3)

            def own_tiles(c, row):
                act.wait_ge(W["moments"], (2 * c + row // 2 + 1) * NORM(CHUNK))
                for s in range(c * CHUNK, (c + 1) * CHUNK):
                    if row == 0:
                        normalized(xn_all[:, s], s, row).then_inc(W["norm1_part"], 1)
                    else:
                        if c:
                            act.wait_ge(W["zT_ready"], s - CHUNK + 1)
                        normalized(zb[:, s % CHUNK], s, row).then_inc(W["zb_part"], 1)

            def keep_block_qkv(s):
                if s >= 2:
                    act.wait_ge(W["bqkv_ready"], s - 1)
                act.wait_ge(W["zT_ready"], s + 1)
                A.activation(lnT[:, s % 2, :], bank[s % 2][:], ACT.Identity, bias=C["ln1b"][:], scale=C["ln1w"][:]).then_inc(W["lnT_done"], 1)
                if s:
                    keep_qkv(s - 1)

            def keep_qkv(s):
                act.wait_ge(W["bqkv_ready"], s + 1)
                for k in range(2):
                    i = A.copy(qkv_t[:, s, 2 * k:2 * k + 2, :], bank[2 + 2 * (s % 2) + k][:, 0:2 * QKV].rearrange("p (a c) -> p a c", a=2))
                i.then_inc(W["bqkv_done"], 1)

            for row in (0, 2):
                root(0, row)
                own_tiles(0, row)
            act.wait_ge(W["consts_in"], n_consts)
            root(1, 0)
            keep_block_qkv(0)
            own_tiles(1, 0)
            keep_block_qkv(1)
            keep_block_qkv(2)
            root(1, 2)
            keep_block_qkv(3)
            own_tiles(1, 2)
            for s in range(CHUNK, S):
                keep_block_qkv(s)
            keep_qkv(S - 1)
            n = 4 * NORM(CHUNK)

            def copy_normed(half, par, steady):
                s = ev(half, par)
                if steady:
                    act.wait_ge(W["xnT_ready"], s - 1)
                A.copy(xnb[:, par], xn_all[:, s]).then_inc(W["xnb_done"], 1)

            def exponentials_of_unit(half, par):
                act.wait_ge(W["s_diff"], ev(half, par) + 1)
                A.activation(sc2, sc2, ACT.Exp, scale=SCALE).then_inc(W["s_exp"], 1)

            def keep_turned(half, par, steady):
                s = ev(half, par)
                if steady:
                    act.wait_ge(W["q_ready"], s - 1)
                act.wait_ge(W["xnT_ready"], s + 1)
                A.copy(xnT[:, par, :], bank[2][:]).then_inc(W["xnT_done"], 1)

            def keep_projections(half, par, steady):
                s = ev(half, par)
                if steady:
                    act.wait_ge(W["v_ready"], s - 1)
                act.wait_ge(W["lat_ready"], s + 1)
                A.activation(latT[0:LAT, par, :], bank[4][0:LAT, :], ACT.Identity, bias=C["bdown"][:]).then_inc(W["lat_done"], 1)
                act.wait_ge(W["q_ready"], s + 1)
                A.copy(q_all[:, s, :], bank[3][:]).then_inc(W["q_done"], 1)
                act.wait_ge(W["k_ready"], s + 1)
                A.copy(k_all[:, s, :], bank[6][:]).then_inc(W["k_done"], 1)
                act.wait_ge(W["v_ready"], s + 1)
                A.copy(v_all[:, s, :], bank[7][:]).then_inc(W["v_done"], 1)

            def second_stage(half, par, steady):
                copy_normed(half, par, steady)
                exponentials_of_unit(half, par)
                keep_turned(half, par, steady)
                if steady or par:
                    keep_sums(half if par else half - 1, 1 - par)
                keep_projections(half, par, steady)

            def keep_sums(half, par):
                u = ev(half, par)
                at = 2 * par * GW
                act.wait_ge(W["pv_ready"], u + 1)
                A.copy(qkv_t[:, :, half, at:at + 2 * GW].rearrange("p s (l w) -> p l s w", l=2)[:, :, :, 0:QH * HD],
                       bank[1][:].rearrange("p (l s w) -> p l s w", l=2, s=S)).then_inc(W["block_kept"], 1)

            act.wait_ge(W["zb_done"], S)
            act.wait_ge(W["zT_ready"], S)
            in_pairs(act, second_stage, EARLY)
            for u in range(EARLY, S):
                copy_normed(u // 2, u % 2, True)
                exponentials_of_unit(u // 2, u % 2)
                keep_sums((u - 1) // 2, 1 - u % 2)
            keep_sums(S // 2 - 1, 1)

            def copy_block(half, par, steady):
                s = ev(half, par)
                if steady:
                    act.wait_ge(W["bT_ready"], s - 1)
                A.copy(aoc[:, par].rearrange("p a (g w) -> p a g w", g=G),
                       qkv_t[:, s].rearrange("p a (g w) -> p a g w", g=G)[:, :, :, 0:QH * HD]).then_inc(W["aoc_done"], 1)

            def keep_block(half, par, steady):
                s = ev(half, par)
                act.wait_ge(W["bT_ready"], s + 1)
                wait_past(act, "proj_ready", s)
                A.copy(bT, bank[par][:]).then_inc(W["bT_done"], 1)

            act.wait_ge(W["block_kept"], S)
            staggered(act, copy_block, keep_block)
            deviation(0, S, 0, n + S + 3)

            act.wait_ge(W["moments"], n + NORM(S))
            act.wait_ge(W["aoc_done"], S)
            normalized(z2_all[:, 0], 0, 0).then_inc(W["z2_part"], 1)
            for s in range(S):
                if s + 1 < S:
                    normalized(z2_all[:, s + 1], s + 1, 0).then_inc(W["z2_part"], 1)
                act.wait_ge(W["z2T_ready"], s + 1)
                if s >= 2:
                    act.wait_ge(W["logit_ready"], s - 1)
                A.activation(lnT[:, s % 2, :], bank[4 + 3 * (s % 2)][:], ACT.Identity, bias=C["ln2b"][:], scale=C["ln2w"][:]).then_inc(W["x2T_done"], 1)

            def exponentials(s, par):
                act.wait_ge(W["row_diff"], s + 1)
                A.activation(score[:, par, :], score[:, par, :], ACT.Exp, scale=SCALE).then_inc(W["row_exp"], 1)

            exponentials(0, 0)
            act.wait_ge(W["tot_ready"], 1)
            A.copy(tot16[:], bank[1][:, 0:NT * E]).then_inc(W["tot_kept"], 1)
            act.wait_ge(W["diff_done"], 1)
            A.activation(gate[:, 1, :], tmp1[:], ACT.Exp).then_inc(W["route_exp"], 1)
            for s in range(EARLY, S):
                keep_turned(s // 2, s % 2, True)
                keep_projections(s // 2, s % 2, True)
            act.wait_ge(W["index_done"], 1)

            def expert(half, par):
                e = ev(half, par)
                wait_past(act, "part_ready", PARTS * e)
                for m, (at, n) in enumerate(chunks):
                    act.wait_ge(W["part_ready"], PARTS * e + m + 1)
                    A.activation(xeT[:, at:at + n], bank[m % BANKS][:, 0:n], ACT.Identity, bias=C["ln2b"][:], scale=C["ln2w"][:]).then_inc(W["part_kept"], 1)
                for f in range(FH):
                    for m, (at, n) in enumerate(chunks):
                        k = 3 + 3 * f + m
                        act.wait_ge(W["part_ready"], PARTS * e + k + 1)
                        A.activation(hT[:, f, at:at + n], bank[k % BANKS][:, 0:n], ACT.Gelu_apprx_tanh).then_inc(W["part_kept"], 1)
                wait_past(act, ye_out[par], 48 * half)
                for q in range(3):
                    k = 3 + 3 * FH + q
                    n = min(4, CT - 4 * q)
                    act.wait_ge(W["part_ready"], PARTS * e + k + 1)
                    A.copy(ye[:, par, 4 * q:4 * q + n, :], bank[k % BANKS][:, 0:n * D].rearrange("p (a d) -> p a d", d=D)).then_inc(W["part_kept"], 1)

            def keep_attention(s):
                act.wait_ge(W["ao_ready"], s + 1)
                wait_past(act, "attn_ready", s)
                A.copy(aoT[:], bank[4][:]).then_inc(W["aoT_done"], 1)

            def attention(s, par):
                if not isinstance(s, int) or s >= 1:
                    keep_attention(s - 1)

            def next_exponentials(s, par):
                if not isinstance(s, int) or s > 0:
                    exponentials(s, par)

            fourth(act, next_exponentials, expert, attention)

            def silu(half, par, steady):
                s = ev(half, par)
                act.wait_ge(W["f_step"], TOPK * (s + 1))
                if steady:
                    act.wait_ge(W["res_done"], s - 1)
                A.activation(gb[:, par], xn_all[:, s], ACT.Silu).then_inc(W["silu_done"], 1)

            in_pairs(act, silu, S // 2)
            keep_attention(S - 1)
            with act.Fori(S // 4, S // 2) as half:
                silu(half, 0, True)
                silu(half, 1, True)

        @block.gpsimd
        def _(pool):
            Q = nc.gpsimd
            pool.wait_ge(W["consts_in"], n_consts)
            def key_products(half, par, steady):
                u = ev(half, par)
                if steady:
                    pool.wait_ge(W["qk_score"], u - 1)
                if steady or par:
                    key_product(Q, half, par, 0, range(OWN_KEYS.stop, S))
                i = key_product(Q, half, par, 1, range(S))
                i.then_inc(W["qk_prod"], 1)

            def own_values(half, par, steady):
                u = ev(half, par)
                if steady:
                    pool.wait_ge(W["pv_ready"], u - 1)
                pool.wait_ge(W["s_prob"], u + 1)
                value_products(Q, half, par, 1).then_inc(W["pv_prod"], 1)

            pool.wait_ge(W["bqkv_done"], S)
            pool.wait_ge(W["filled"], 1)
            staggered(pool, key_products, own_values)

            def help_scores(s, par):
                kind = s if isinstance(s, int) else LOOP.start
                if kind > 1:
                    pool.wait_ge(W["score_done"], s)
                for a in range(TT - HELPED_QK[kind], TT):
                    qk_product(Q, help_buf[kind][a], s, par, a).then_inc(W["help_qk"], 1)

            def help_values(s, par):
                if not eager(s):
                    pool.wait_ge(W["value_sum"], s)
                if not isinstance(s, int) or s > FEW_IN[0]:
                    pool.wait_ge(W["value_part"], few_before(s))
                pool.wait_ge(W["row_exp"], s + 1)
                for a in range(TT - HELPED_PV[s if isinstance(s, int) else 3], TT):
                    pv_product(Q, s, par, a).then_inc(W["help_pv"], 1)

            turned = 0

            def rotate(v, s):
                nonlocal turned
                with_cos, with_sin = (late_buf if s >= EARLY else turned_buf)[turned % 2]
                if turned >= 2:
                    pool.wait_ge(W["turned"], turned - 1)
                turn(Q, v, s, with_cos, with_sin).then_inc(W["turn_step"], 1)
                turned += 1
                pool.wait_ge(W["turn_step"], turned)
                Q.tensor_tensor(v[:, s, :], with_cos, with_sin, ALU.add).then_inc(W["turned"], 1)

            pool.wait_ge(W["q_done"], EARLY)
            pool.wait_ge(W["k_done"], EARLY)
            rotate(k_all, 1)
            rotate(q_all, 1)
            pool.wait_ge(W["own_turned"], 2)
            pool.wait_ge(W["pv_ready"], S)
            pool.wait_ge(W["qk_score"], S)
            help_scores(0, 0)
            pool.wait_ge(W["turned"], turned)
            help_scores(1, 1)
            for s in range(2, EARLY):
                rotate(k_all, s)
                rotate(q_all, s)

            pool.wait_ge(W["zero_out"], 16 * CT)
            pool.wait_ge(W["index_done"], 1)
            pool.wait_ge(W["z2_done"], S)
            pool.wait_ge(W["z2_part"], S)
            for k in range(TOPK):
                for n in range(NT):
                    Q.indirect_dma_start(slots_d, bass.IndirectOffsetOnAxis(ap=scatter_at[:, k, n:n + 1], axis=0),
                                         z2_all[:, n // TT, n % TT, :], None).then_inc(W["scattered"], 16)
            pool.wait_ge(W["q_done"], S)
            pool.wait_ge(W["k_done"], S)
            pool.wait_ge(W["v_done"], S)
            pool.wait_ge(W["scattered"], 16 * NT * TOPK)
            help_values(2, 0)
            with pool.Fori(1, S // 2 - 2) as half:
                for par in (1, 0):
                    s = 2 * half + 2 - par
                    help_scores(s + 1, 1 - par)
                    help_values(s, par)
            rotate(k_all, S - 2)
            rotate(q_all, S - 2)
            pool.wait_ge(W["turned"], turned)
            help_scores(S - 2, 0)
            help_values(S - 3, 1)
            rotate(k_all, S - 1)
            rotate(q_all, S - 1)

            for par in range(2):
                pool.wait_ge(ye_out[par], 48 * (E // 2))
            for s in range(S):
                if s >= 2:
                    pool.wait_ge(gathered[s % 2], 16 * TT * TOPK * (s // 2))
                for a in range(TT):
                    for k in range(TOPK):
                        n = s * TT + a
                        Q.indirect_dma_start(yg[:, s, a, k, :], None, expert_d,
                                             bass.IndirectOffsetOnAxis(ap=gather_at[:, k, n:n + 1], axis=0)).then_inc(gathered[s % 2], 16)


def kernel(L0_attn_x, L0_attn_Wq, L0_attn_bq, L0_attn_Wdown, L0_attn_bdown, L0_attn_Wup, L0_attn_bup, L0_attn_Wout,
           L0_attn_bout, L0_ffn_ln1_weight, L0_ffn_ln1_bias, L0_ffn_ln2_weight, L0_ffn_ln2_bias, L0_ffn_qkv_weight,
           L0_ffn_proj_weight, L0_ffn_router_weight, L0_ffn_moe_w1, L0_ffn_moe_w2):
    import concourse.bacc as bacc
    import ml_dtypes
    from concourse.bass_utils import run_bass_kernel_spmd

    wup = np.concatenate([np.asarray(L0_attn_Wup), np.asarray(L0_attn_bup)[None]]).reshape(LAT + 1, H, 2, HD)
    col = lambda v: np.asarray(v).reshape(-1, 1)
    own = np.ascontiguousarray

    freq = (1.0 / 10000.0 ** (np.arange(0, HD, 2, dtype=np.float32) / np.float32(HD))).astype(np.float32)
    angle = (np.arange(T, dtype=np.float32)[:, None] * freq).reshape(TT, P, 1, 1, HD // 2).transpose(1, 0, 2, 3, 4)
    table = lambda first, second: own(np.broadcast_to(np.concatenate([first, second], 3), (P, TT, H, 2, HD // 2)), np.float32).reshape(P, TT * D)
    bf16 = ml_dtypes.bfloat16
    token = np.arange(NT)[None, None, :] * P + np.arange(P)[:, None, None]
    arrays = dict(
        x=np.asarray(L0_attn_x), wq=np.asarray(L0_attn_Wq), bq=np.asarray(L0_attn_bq)[None], wdown=np.asarray(L0_attn_Wdown),
        bdown=col(L0_attn_bdown), wupk=own(wup[:, :, 0].reshape(LAT + 1, D)), wupv=own(wup[:, :, 1].transpose(0, 2, 1)).reshape(LAT + 1, D),
        wout=np.asarray(L0_attn_Wout), bout=np.asarray(L0_attn_bout),
        ln1w=col(L0_ffn_ln1_weight), ln1b=col(L0_ffn_ln1_bias), ln2w=col(L0_ffn_ln2_weight), ln2b=col(L0_ffn_ln2_bias),
        wqkv=own(np.asarray(L0_ffn_qkv_weight).T), wproj=own(np.asarray(L0_ffn_proj_weight).T),
        wrouter=np.asarray(L0_ffn_router_weight), w1=np.asarray(L0_ffn_moe_w1), w2=np.asarray(L0_ffn_moe_w2),
        cos=table(np.cos(angle), np.cos(angle)), sin=table(-np.sin(angle), np.sin(angle)),
        identf=np.eye(P, dtype=np.float32), ones1=np.ones((1, P), np.float32),
        earlier=own(np.kron(np.triu(np.ones((NT, NT), np.float32), 1), np.eye(E, dtype=np.float32))
                    .reshape(HALVES, P, NT * E).transpose(1, 0, 2)).reshape(P, -1).astype(bf16),
        tri=np.triu(np.ones((P, P), np.float32), 1).astype(bf16), allones=np.ones((P, P), bf16),
        rev8=np.tile(np.arange(E, 0, -1, dtype=np.float32), (P, 1)),
        ebase=np.tile(np.arange(E, dtype=np.float32) * CAP, (P, 1)),
        dump=(SLOTS + TOPK * token + np.arange(TOPK)[None, :, None]).reshape(P, -1).astype(np.float32),
    )
    nc = bacc.Bacc("TRN2", target_bir_lowering=False, num_devices=1)
    aps = {n: nc.dram_tensor(f"in_{n}", a.shape, mybir.dt.from_np(a.dtype), kind="ExternalInput").ap() for n, a in arrays.items()}
    out = nc.dram_tensor("out", (S, T, D), F32, kind="ExternalOutput").ap()
    build(nc, **aps, out=out)
    r = run_bass_kernel_spmd(nc, [{f"in_{n}": a for n, a in arrays.items()}], core_ids=[0])
    return r.results[0]["out"]
```
